# Optimizing a Trainium2 kernel written in Bass

```python
import numpy as np
import jax
import jax.numpy as jnp

def _softmax(x, axis=-1):
    return jax.nn.softmax(x, axis=axis)
def _gelu(x):
    return jax.nn.gelu(x, approximate=True)
def _silu(x):
    return jax.nn.silu(x)
def _sigmoid(x):
    return jax.nn.sigmoid(x)
def _layernorm(x, axis=-1, eps=1e-5):
    m = jnp.mean(x, axis=axis, keepdims=True)
    v = jnp.var(x, axis=axis, keepdims=True)
    return (x - m) / jnp.sqrt(v + eps)
def _scatter_add(tgt, idx, src, axis=0):
    return tgt.at[idx].add(src)
def _segment_sum(src, seg, n):
    return jax.ops.segment_sum(src, seg, n)

kernel_name = 'mk_conv_attn_hybrid_d2_conv_nchw128_f0c822'

def setup_inputs(seed: int = 0):
    np.random.seed(seed)
    _w = jnp.asarray
    def _rec_inputs():
        import jax
        import jax.numpy as jnp
        _gk = jax.random.key(seed)
        x = -0.0006537 + 1.001 * jax.random.normal(jax.random.fold_in(_gk, 1), (8, 128, 48, 48), jnp.float32)
        return x
    x = _rec_inputs()
    def _L0_conv_setup():
        import jax, jax.numpy as jnp
        import numpy as np
        B, C, H, W = (8, 128, 48, 48)
        RED = 16
        key = jax.random.key(seed)
        ks = jax.random.split(key, 8)
        s = 0.05
        return {'x': jax.random.normal(ks[0], (B, C, H, W), jnp.float32), 'Wq': jax.random.normal(ks[1], (C, C), jnp.float32) * s, 'bq': jnp.zeros((C,), jnp.float32), 'Wk': jax.random.normal(ks[2], (C, C), jnp.float32) * s, 'bk': jnp.zeros((C,), jnp.float32), 'Wv': jax.random.normal(ks[3], (C, C), jnp.float32) * s, 'bv': jnp.zeros((C,), jnp.float32), 'se_w1': jax.random.normal(ks[4], (C // RED, C), jnp.float32) * s, 'se_w2': jax.random.normal(ks[5], (C, C // RED), jnp.float32) * s, 'gamma': jax.random.normal(ks[6], (1,), jnp.float32)}
    _L0_conv_all = _L0_conv_setup()
    _L0_conv_in = {k: v for k, v in _L0_conv_all.items() if k in ('Wq', 'bq', 'Wk', 'bk', 'Wv', 'bv', 'se_w1', 'se_w2', 'gamma', )}
    del _L0_conv_all

    def _L1_attn_setup():
        import jax, jax.numpy as jnp
        import numpy as np
        key = jax.random.key(seed)
        seq = jax.random.normal(key, (32, 2048, 128), dtype=jnp.float32)
        return {'seq': seq}
    _L1_attn_all = _L1_attn_setup()
    _L1_attn_in = {k: v for k, v in _L1_attn_all.items() if k in ()}
    del _L1_attn_all

    def _L1_ffn_setup():
        import jax, jax.numpy as jnp
        import numpy as np
        B, N, D, C, E, K = (8, 8192, 128, 128, 8, 2)
        key = jax.random.key(seed)
        k0, k1, k2 = jax.random.split(key, 3)
        x = jax.random.normal(k0, (B, N, D), dtype=jnp.float32)
        router_w = jax.random.normal(k1, (D, E), dtype=jnp.float32) * 0.05
        router_b = jnp.zeros((E,), dtype=jnp.float32)
        expert_w = jax.random.normal(k2, (E, D, C), dtype=jnp.float32) * (1.0 / np.sqrt(D))
        expert_b = jnp.zeros((E, C), dtype=jnp.float32)
        return {'x': x, 'router_w': router_w, 'router_b': router_b, 'expert_w': expert_w, 'expert_b': expert_b}
    _L1_ffn_all = _L1_ffn_setup()
    _L1_ffn_in = {k: v for k, v in _L1_ffn_all.items() if k in ('router_w', 'router_b', 'expert_w', 'expert_b', )}
    del _L1_ffn_all

    return {
        "x": x,
        "L0_conv_Wq": _L0_conv_in["Wq"],
        "L0_conv_bq": _L0_conv_in["bq"],
        "L0_conv_Wk": _L0_conv_in["Wk"],
        "L0_conv_bk": _L0_conv_in["bk"],
        "L0_conv_Wv": _L0_conv_in["Wv"],
        "L0_conv_bv": _L0_conv_in["bv"],
        "L0_conv_se_w1": _L0_conv_in["se_w1"],
        "L0_conv_se_w2": _L0_conv_in["se_w2"],
        "L0_conv_gamma": _L0_conv_in["gamma"],
        "L1_ffn_router_w": _L1_ffn_in["router_w"],
        "L1_ffn_router_b": _L1_ffn_in["router_b"],
        "L1_ffn_expert_w": _L1_ffn_in["expert_w"],
        "L1_ffn_expert_b": _L1_ffn_in["expert_b"],
    }

def reference(x, L0_conv_Wq, L0_conv_bq, L0_conv_Wk, L0_conv_bk, L0_conv_Wv, L0_conv_bv, L0_conv_se_w1, L0_conv_se_w2, L0_conv_gamma, L1_ffn_router_w, L1_ffn_router_b, L1_ffn_expert_w, L1_ffn_expert_b):
    import jax
    import jax.numpy as jnp
    def _L0_conv_ref(x, Wq, bq, Wk, bk, Wv, bv, se_w1, se_w2, gamma):
        import jax, jax.numpy as jnp
        import numpy as np
        B, C, H, W = (8, 128, 48, 48)
        RED = 16
        b, c, h, w = x.shape
        n = h * w
        xf = x.reshape(b, c, n)
        q = jnp.einsum('oc,bcn->bon', Wq, xf) + bq[None, :, None]
        k = jnp.einsum('oc,bcn->bon', Wk, xf) + bk[None, :, None]
        v = jnp.einsum('oc,bcn->bon', Wv, xf) + bv[None, :, None]
        energy = jnp.einsum('bci,bcj->bij', q, k)
        attn = jax.nn.softmax(energy, axis=-1)
        out = jnp.einsum('bcj,bij->bci', v, attn).reshape(b, c, h, w)
        y = jnp.mean(x, axis=(2, 3))
        y = jax.nn.relu(y @ se_w1.T)
        y = jax.nn.sigmoid(y @ se_w2.T)
        x_se = x * y[:, :, None, None]
        return gamma[0] * out + x_se

    def _L1_attn_ref(seq):
        import jax, jax.numpy as jnp
        import numpy as np
        attn = jnp.einsum('blc,bmc->blm', seq, seq)
        attn = jax.nn.softmax(attn, axis=2)
        out = jnp.einsum('blm,bmc->blc', attn, seq)
        return out

    def _L1_ffn_ref(x, router_w, router_b, expert_w, expert_b):
        import jax, jax.numpy as jnp
        import numpy as np
        B, N, D, C, E, K = (8, 8192, 128, 128, 8, 2)
        router_probs = jax.nn.softmax(x @ router_w + router_b, axis=-1)
        top_p, top_i = jax.lax.top_k(router_probs, K)
        top_p = top_p / jnp.sum(top_p, axis=-1, keepdims=True)
        expert_out = jnp.einsum('bnd,edc->bnec', x, expert_w) + expert_b
        gathered = jnp.take_along_axis(expert_out, top_i[..., None], axis=2)
        return jnp.einsum('bnk,bnkc->bnc', top_p, gathered)

    def _gn(v, G=32, eps=1e-5):
        B_, C_, H_, W_ = v.shape
        g = v.reshape(B_, G, C_ // G, H_, W_)
        m = jnp.mean(g, axis=(2, 3, 4), keepdims=True)
        s = jnp.var(g, axis=(2, 3, 4), keepdims=True)
        return ((g - m) / jnp.sqrt(s + eps)).reshape(v.shape)

    def _ln_c(v, eps=1e-6):
        m = jnp.mean(v, axis=1, keepdims=True)
        s = jnp.var(v, axis=1, keepdims=True)
        return (v - m) / jnp.sqrt(s + eps)

    def _ln_t(v, eps=1e-5):
        m = jnp.mean(v, axis=-1, keepdims=True)
        s = jnp.var(v, axis=-1, keepdims=True)
        return (v - m) / jnp.sqrt(s + eps)

    def _to_tokens(v):
        B_, C_, H_, W_ = v.shape
        return v.reshape(B_, C_, H_ * W_).transpose(0, 2, 1)
    def _from_tokens(t, like):
        B_, C_, H_, W_ = like.shape
        return t.transpose(0, 2, 1).reshape(B_, C_, H_, W_)

    x = x + _L0_conv_ref(_gn(x), L0_conv_Wq, L0_conv_bq, L0_conv_Wk, L0_conv_bk, L0_conv_Wv, L0_conv_bv, L0_conv_se_w1, L0_conv_se_w2, L0_conv_gamma)
    t = _to_tokens(x)
    t = t + _L1_attn_ref(_ln_t(t))
    t = t + _L1_ffn_ref(_ln_t(t), L1_ffn_router_w, L1_ffn_router_b, L1_ffn_expert_w, L1_ffn_expert_b)
    x = _from_tokens(t, x)
    return x


_drawn_inputs = setup_inputs


def setup_inputs(seed=0):
    import zlib

    import numpy as np

    out = dict(_drawn_inputs(seed))
    spreads = {'L0_conv_bq': (0.0, 0.1),
     'L0_conv_bk': (0.0, 2.0),
     'L0_conv_bv': (0.0, 0.1),
     'L1_ffn_router_b': (0.0, 0.1),
     'L1_ffn_expert_b': (0.0, 0.296)}
    factors = {'L0_conv_se_w1': 21.376, 'L0_conv_se_w2': 8.0}
    for name, (base, spread) in spreads.items():
        noise = np.random.default_rng([zlib.crc32(name.encode()), seed]).standard_normal(out[name].shape)
        drawn = base * np.exp(spread * noise) if base else spread * noise
        out[name] = jnp.asarray(drawn.astype(out[name].dtype))
    for name, factor in factors.items():
        out[name] = (out[name] * factor).astype(out[name].dtype)
    return out
```

```python
import concourse.bass as bass
from concourse import mybir
from contextlib import ExitStack

F32 = mybir.dt.float32
F32R = mybir.dt.float32r
ALU = mybir.AluOpType
ACT = mybir.ActivationFunctionType
AX = mybir.AxisListType

B, C, NTOK = 8, 128, 48 * 48
E, RED = 8, 8
TILE = 128
NT = NTOK // TILE
BW = 3 * TILE
NB = NTOK // BW
TPB = BW // TILE
LW = 2 * BW
LB = NTOK // LW
QC = [(0, 1024), (1024, 1024), (2048, NTOK - 2048)]
GN_EPS, LN_EPS = 1e-5, 1e-5
SHIFT = C / 2.0
LAG = 2
PTS = NTOK // BW
RING0 = 6


def chunk_of(j):
    end = (j + 1) * TILE
    return next(c for c, (a, w) in enumerate(QC) if end <= a + w)


def plan():
    s = [("gn",), ("xg", 0), ("xg", 1), ("xg", 2), ("base",)]
    for m in range(NB):
        s += [("kproj", m), ("vproj", m), ("baset", m), ("vt", m)]
    s += [("qproj", 0)]
    later = []
    for n in range(NB + 1):
        for j in range(NT):
            r, q = divmod(j, 6)
            if n >= 1:
                s.append(("pt", n - 1, j))
                g = (n - 1) * NT + j - LAG
                if g >= 0:
                    s.append(("pv", g // NT, g % NT))
            if n >= 2:
                m = n - 2
                s += {2: [("oevac", m)], 4: [("ot", m)], 6: [("ln", m)], 8: [("lnapply", m)], 11: [("tnt", m)]}.get(j, [])
            if n < NB:
                s.append(("scores", n, r, q) if q < 3 else ("exp", n, r, q - 3))
                if n + 1 < NB and j == 12:
                    s.append(("qproj", n + 1))
    m = NB - 1
    tail = {0: [("pv", m, NT - 2)], 1: [("pv", m, NT - 1)], 2: [("oevac", m)], 3: [("ot", m)], 4: [("ln", m)],
            5: [("lnapply", m)], 8: [("tnt", m)]}
    for w in range(LB * NT):
        s.append(("s1", w))
        s += tail.get(w, [])
        if w >= LAG:
            s.append(("pv1", w - LAG))
            if (w - LAG) % NT == NT - 1:
                s.append(("o1evac", (w - LAG) // NT))
    for w in range(LB * NT - LAG, LB * NT):
        s.append(("pv1", w))
    s += [("o1evac", LB - 1), ("rd1",)]
    s += [("o1t", 0), ("uln", 0), ("uapply", 0), ("ut", 0), ("router", 0)]
    for mb in range(NB):
        for k in range(TPB):
            s += [("expert", mb, k, 0), ("expert", mb, k, 1)]
            if mb + 1 < NB:
                s += {0: [("o1t", mb + 1), ("uln", mb + 1)], 1: [("uapply", mb + 1)]}.get(k, [])
        if mb + 1 < NB:
            s += [("ut", mb + 1), ("router", mb + 1)]
        s += [("yt", mb)]
    return s


PLAN = plan()
RAISES = {
    "gn": ["gn_stats_ready", "ring_full", "gn_dev_ready", "ring_full", "gn_var_ready", "gn_rstd_ready", "se_in_ready", "ring_full", "se_hidden_ready",
           "ring_full", "se_exp_ready"],
    "xg": ["xg_norm_ready", "xg_hi_ready", "xg_lo_ready"], "base": ["base_done"],
    "kproj": ["ring_full", "k_hi_ready", "k_lo_ready"], "vproj": ["ring_full", "v_chan_ready"], "vt": ["ring_full", "v_hi_ready", "v_lo_ready"],
    "baset": ["ring_full", "base_tok_ready"], "qproj": ["ring_full", "q_hi_ready", "q_lo_ready"],
    "scores": ["scores_done", "row_max_ready"], "exp": ["p_rows_ready"],
    "pt": ["ring_full", "pt_hi_ready", "pt_lo_ready"], "pv": ["pv_done"], "oevac": ["o_chan_ready"],
    "ot": ["ring_full", "o_added"], "ln": ["ln_var_ready", "ln_rstd_ready"], "lnapply": ["tn_tok_ready", "tn_hi_ready", "tn_lo_ready"],
    "tnt": ["ring_full", "tnt_hi_ready", "tnt_lo_ready"],
    "s1": ["s1_done", "p1_exp_ready", "p1_hi_ready", "p1_lo_ready"], "pv1": ["pv1_done"], "o1evac": ["o1_chan_ready"], "rd1": ["r1_done"],
    "o1t": ["ring_full", "o1_added"], "uln": ["u_var_ready", "u_rstd_ready"], "uapply": ["u_tok_ready"],
    "ut": ["ring_full", "u_hi_ready", "u_lo_ready"], "router": ["ring_full", "logit_max_ready", "gate_exp_ready", "gates_ready"],
    "expert": ["ring_full", "expert_added"], "yt": ["ring_full", "y_chan_ready"],
}
LAST = {"kproj": "k_lo_ready", "vproj": "v_chan_ready", "vt": "v_lo_ready", "baset": "base_tok_ready", "qproj": "q_lo_ready", "pt": "pt_lo_ready",
        "ot": "o_added", "tnt": "tnt_lo_ready", "o1t": "o1_added", "ut": "u_lo_ready", "router": "logit_max_ready",
        "expert": "expert_added", "yt": "y_chan_ready"}
GN_LAST = ["gn_dev_ready", "gn_var_ready", "se_hidden_ready", "se_exp_ready"]

ORDER = {}
RING = []
for _step in PLAN:
    _turn = 0
    for _sem in RAISES[_step[0]]:
        if _sem == "ring_full":
            _key = _step + (_turn,)
            RING.append((_step, GN_LAST[_turn] if _step[0] == "gn" else LAST[_step[0]]))
            _turn += 1
        else:
            _key = _step
        ORDER.setdefault(_sem, {})[_key] = len(ORDER.setdefault(_sem, {})) + 1
PER = {sem: len(keys) for sem, keys in ORDER.items()}
assert len(RING) % 2 == 0 and len(RING) == PER["ring_full"]
STARTED = {"ring_full", "p1_lo_ready", "p1_hi_ready", "p1_exp_ready", "pv1_done", "o1_chan_ready", "o_added", "r1_done", RING[-1][1], RING[-2][1]}
CHAINED = {"gn": 13, "base": 0, "ot": 5, "ln": 6, "rd1": 1, "o1t": 2, "uln": 6, "router": 11, "expert": 3, "scores": 1,
           "lnapply": 2, "uapply": 2}


def build(nc, x, wq, wk, wv, bq, bk, bv, w1, w2, gamma, rw, rb, ew, eb, y):
    ctx = ExitStack()
    with ctx:
        def sb(name, shape, dt=F32):
            return ctx.enter_context(nc.sbuf_tensor(name, shape, dt))

        ps = ctx.enter_context(nc.psum_tensor("ps", [128, 8, 512], F32))

        ident = sb("ident", [128, 128])
        group = sb("group", [128, 128])
        ones = sb("ones", [128, 128], F32R)
        lower = sb("lower", [128, E, E])
        minus_half = sb("minus_half", [128, TPB])
        shift = sb("shift", [128, 1])
        w_hi = sb("w_hi", [128, 3, 128], F32R)
        w_lo = sb("w_lo", [128, 3, 128], F32R)
        biases = sb("biases", [128, 4])
        w1_sb = sb("w1_sb", [128, RED])
        w2_sb = sb("w2_sb", [RED, 128])
        rw_hi = sb("rw_hi", [128, E], F32R)
        rw_lo = sb("rw_lo", [128, E], F32R)
        rb_sb = sb("rb_sb", [128, E])
        ew_hi = sb("ew_hi", [128, E * 128], F32R)
        ew_lo = sb("ew_lo", [128, E * 128], F32R)
        eb_rows = sb("eb_rows", [128, E * 128], F32R)

        x_chan = sb("x_chan", [128, NTOK])
        t_tok = sb("t_tok", [128, NT, 128])
        xt_hi = sb("xt_hi", [128, NTOK], F32R)
        xt_lo = sb("xt_lo", [128, NTOK], F32R)
        k_hi = sb("k_hi", [128, NTOK], F32R)
        k_lo = sb("k_lo", [128, NTOK], F32R)
        v_hi = sb("v_hi", [128, NT, 128], F32R)
        v_lo = sb("v_lo", [128, NT, 128], F32R)
        q_hi = sb("q_hi", [128, 2, BW], F32R)
        q_lo = sb("q_lo", [128, 2, BW], F32R)
        p_rows = sb("p_rows", [128, 2, TPB, NTOK])
        pt_hi = sb("pt_hi", [128, PTS, BW], F32R)
        pt_lo = sb("pt_lo", [128, PTS, BW], F32R)
        o_chan = sb("o_chan", [128, BW])
        tn_tok = sb("tn_tok", [128, TPB, 128])
        tn_hi = sb("tn_hi", [128, NT, 128], F32R)
        tn_lo = sb("tn_lo", [128, NT, 128], F32R)
        u_tok = sb("u_tok", [128, TPB, 128])
        u_hi = sb("u_hi", [128, BW], F32R)
        u_lo = sb("u_lo", [128, BW], F32R)
        acc = sb("acc", [128, 2, TPB, 128])
        y_out = sb("y_out", [128, 2, BW])
        xg_f = p_rows[:, 0, 0, 0:2 * LW].rearrange("p (s w) -> p s w", s=2)
        v_chan = p_rows[:, 1, 0, 0:2 * BW].rearrange("p (s w) -> p s w", s=2)
        p1_f = p_rows[:, 0, 0, 0:2 * LW].rearrange("p (s w) -> p s w", s=2)
        o1_chan = p_rows[:, 1, 0, :]
        p1_hi = pt_hi[:, :, :].rearrange("p (s a) w -> p s (a w)", a=2)
        p1_lo = pt_lo[:, :, :].rearrange("p (s a) w -> p s (a w)", a=2)
        w_stage = p_rows[:, 0, 0, 0:384].rearrange("p (a w) -> p a w", a=3)
        rw_stage = p_rows[:, 0, 0, 384:384 + E]
        ew_stage = p_rows[:, 0, 1, 0:E * 128]
        eb_stage = p_rows[:, 0, 2, 0:E * 128]
        eb_split = p_rows[:, 1, 0, 0:E * 128]

        wait_carrier = sb("wait_carrier", [128, 1])
        gn_raw = sb("gn_raw", [128, NB, 6])
        gn_mv = sb("gn_mv", [128, 2])
        gs = sb("gs", [128, 12])
        gmean, gdev, gsq, gve, grstd, se_in, se_h, se_e, ysig, yscale, yshift, se_tmp = [gs[:, i:i + 1] for i in range(12)]
        mx = sb("mx", [128, 3])
        negmax = sb("negmax", [128, 2])
        dparts = sb("dparts", [128, NB, TPB, 3])
        rg = sb("rg", [128, 3, TPB])
        ln_raw = sb("ln_raw", [128, TPB, 6])
        ln_mv = sb("ln_mv", [128, TPB, 2])
        ln_ve = sb("ln_ve", [128, TPB])
        ln_rs = sb("ln_rs", [128, TPB])
        d1parts = sb("d1parts", [128, NT, LB])
        r1 = sb("r1", [128, 2, NT])
        u_raw = sb("u_raw", [128, TPB, 6])
        u_mv = sb("u_mv", [128, TPB, 2])
        u_ve = sb("u_ve", [128, TPB])
        u_rs = sb("u_rs", [128, TPB])
        logits = sb("logits", [128, TPB, E])
        centred = sb("centred", [128, TPB, E])
        gexp = sb("gexp", [128, TPB, E])
        lmax = sb("lmax", [128, TPB])
        cmp_gt = sb("cmp_gt", [128, TPB, E, E])
        cmp_ge = sb("cmp_ge", [128, TPB, E, E])
        rank = sb("rank", [128, TPB, E])
        gsum = sb("gsum", [128, 2, TPB])
        gates = sb("gates", [128, 2, TPB, E])

        def signal(name):
            return ctx.enter_context(nc.semaphore(name))

        gn_stats_ready = signal("gn_stats_ready")
        ring_full = signal("ring_full")
        gn_dev_ready = signal("gn_dev_ready")
        gn_var_ready = signal("gn_var_ready")
        gn_rstd_ready = signal("gn_rstd_ready")
        se_in_ready = signal("se_in_ready")
        se_hidden_ready = signal("se_hidden_ready")
        se_exp_ready = signal("se_exp_ready")
        xg_norm_ready = signal("xg_norm_ready")
        xg_hi_ready = signal("xg_hi_ready")
        xg_lo_ready = signal("xg_lo_ready")
        base_done = signal("base_done")
        k_hi_ready = signal("k_hi_ready")
        k_lo_ready = signal("k_lo_ready")
        v_chan_ready = signal("v_chan_ready")
        base_tok_ready = signal("base_tok_ready")
        v_hi_ready = signal("v_hi_ready")
        v_lo_ready = signal("v_lo_ready")
        q_hi_ready = signal("q_hi_ready")
        q_lo_ready = signal("q_lo_ready")
        scores_done = signal("scores_done")
        row_max_ready = signal("row_max_ready")
        p_rows_ready = signal("p_rows_ready")
        pt_hi_ready = signal("pt_hi_ready")
        pt_lo_ready = signal("pt_lo_ready")
        pv_done = signal("pv_done")
        o_chan_ready = signal("o_chan_ready")
        o_added = signal("o_added")
        ln_var_ready = signal("ln_var_ready")
        ln_rstd_ready = signal("ln_rstd_ready")
        tn_tok_ready = signal("tn_tok_ready")
        tn_hi_ready = signal("tn_hi_ready")
        tn_lo_ready = signal("tn_lo_ready")
        tnt_hi_ready = signal("tnt_hi_ready")
        tnt_lo_ready = signal("tnt_lo_ready")
        s1_done = signal("s1_done")
        p1_exp_ready = signal("p1_exp_ready")
        p1_hi_ready = signal("p1_hi_ready")
        p1_lo_ready = signal("p1_lo_ready")
        pv1_done = signal("pv1_done")
        o1_chan_ready = signal("o1_chan_ready")
        r1_done = signal("r1_done")
        o1_added = signal("o1_added")
        u_var_ready = signal("u_var_ready")
        u_rstd_ready = signal("u_rstd_ready")
        u_tok_ready = signal("u_tok_ready")
        u_hi_ready = signal("u_hi_ready")
        u_lo_ready = signal("u_lo_ready")
        logit_max_ready = signal("logit_max_ready")
        gate_exp_ready = signal("gate_exp_ready")
        gates_ready = signal("gates_ready")
        expert_added = signal("expert_added")
        y_chan_ready = signal("y_chan_ready")
        x_loaded = signal("x_loaded")
        w_loaded = signal("w_loaded")
        consts_made = signal("consts_made")
        eb_zeroed = signal("eb_zeroed")
        w_split = signal("w_split")
        vector_chain = signal("vector_chain")
        y_stored = [signal(f"y_stored{i}") for i in range(2)]
        signals = {s.name: s for s in (base_tok_ready, expert_added, gn_dev_ready, gn_var_ready, k_lo_ready,
                                       logit_max_ready, o_added, o1_added, pt_lo_ready, q_lo_ready,
                                       se_exp_ready, se_hidden_ready, tnt_lo_ready, u_lo_ready, v_chan_ready,
                                       v_lo_ready, y_chan_ready)}
        block = ctx.enter_context(nc.Block())

        chain_start, total = {}, 0
        for step in PLAN:
            chain_start[step] = total
            total += CHAINED.get(step[0], 0)
        CHAIN = total
        N_WLOADS = 12
        W_SPLITS = 9

        wait_value = {}

        def value(eng, b, per_batch, count):
            if isinstance(b, int):
                return b * per_batch + count
            if eng.engine not in wait_value:
                wait_value[eng.engine] = eng.alloc_register("wait_value")
            eng.reg_mul(wait_value[eng.engine], b, per_batch)
            eng.reg_add(wait_value[eng.engine], wait_value[eng.engine], count)
            return wait_value[eng.engine]

        def at(eng, b, sem, *step):
            return value(eng, b, PER[sem.name], ORDER[sem.name][step] + (sem.name in STARTED))

        def before(eng, b, sem):
            return value(eng, b, PER[sem.name], 1)

        def ring_index(step, turn=0):
            return ORDER["ring_full"][step + (turn,)] - 1

        def ring_bank(step, turn=0):
            return ps[:, RING0 + ring_index(step, turn) % 2, :]

        def filled(eng, b, step, turn=0):
            return value(eng, b, PER["ring_full"], ring_index(step, turn) + 2)

        def reader(step, turn=0):
            return signals[RING[ring_index(step, turn) - 2][1]]

        def freed(eng, b, step, turn=0):
            i = ring_index(step, turn)
            return at(eng, b, reader(step, turn), *RING[i - 2][0]) if i >= 2 else before(eng, b, reader(step, turn))

        def chained(b, step, links):
            return value(nc.vector, b, CHAIN, chain_start[step] + links)

        def tiled(ap):
            return ap.rearrange("p (t w) -> p t w", w=128)

        @block.sync
        def _(sp):
            for stored in y_stored:
                sp.sem_inc(stored, 1)
            sp.dma_start(x_chan[:, :], x[0]).then_inc(x_loaded, 16)
            sp.dma_start(w_stage[:, 0, :], wq).then_inc(w_loaded, 16)
            sp.dma_start(w_stage[:, 1, :], wk).then_inc(w_loaded, 16)
            sp.dma_start(w_stage[:, 2, :], wv).then_inc(w_loaded, 16)
            sp.dma_start(biases[:, 0:1], bq).then_inc(w_loaded, 16)
            sp.dma_start(biases[:, 1:2], bk).then_inc(w_loaded, 16)
            sp.dma_start(biases[:, 2:3], bv).then_inc(w_loaded, 16)
            sp.dma_start(biases[:, 3:4], gamma).then_inc(w_loaded, 16)
            sp.dma_start(w1_sb[:, :], w1).then_inc(w_loaded, 16)
            sp.dma_start(w2_sb[:, :], w2).then_inc(w_loaded, 16)
            sp.dma_start(rw_stage, rw).then_inc(w_loaded, 16)
            sp.dma_start(rb_sb[:, :], rb).then_inc(w_loaded, 16)
            sp.dma_start(ew_stage, ew).then_inc(w_loaded, 16)
            sp.wait_ge(eb_zeroed, 1)
            sp.dma_start(eb_stage[0:1, :], eb).then_inc(w_loaded, 16)
            sp.dma_start(eb_stage[32:33, :], eb).then_inc(w_loaded, 16)

            def store(b):
                for mb in range(NB):
                    sp.wait_ge(y_chan_ready, at(sp, b, y_chan_ready, "yt", mb))
                    sp.dma_start(y[bass.ds(b, 1), :, mb * BW:(mb + 1) * BW].rearrange("a c n -> (a c) n"),
                                 y_out[:, mb % 2, :]).then_inc(y_stored[mb % 2], 16)

            with sp.Fori(0, B - 1) as b:
                sp.wait_ge(ring_full, filled(sp, b, ("baset", NB - 1)))
                sp.dma_start(x_chan[:, :], x[bass.ds(b + 1, 1)].rearrange("a c n -> (a c) n")).then_inc(x_loaded, 16)
                store(b)
            store(B - 1)
            for stored in y_stored:
                sp.wait_ge(stored, 16 * B * (NB // 2) + 1)

        @block.gpsimd
        def _(pool):
            pool.memset(ident[:, :], 0.0).then_inc(consts_made, 1)
            pool.memset(group[:, :], 1.0 / 4).then_inc(consts_made, 1)
            pool.memset(lower[:, :, :], 1.0).then_inc(consts_made, 1)
            pool.memset(minus_half[:, :], -0.5).then_inc(consts_made, 1)
            pool.memset(shift[:, :], -SHIFT).then_inc(consts_made, 1)
            pool.wait_ge(consts_made, 5)
            pool.affine_select(out=ident[:, :], in_=ident[:, :], compare_op=ALU.not_equal, fill=1.0, base=0,
                               pattern=[[-1, 128]], channel_multiplier=1).then_inc(consts_made, 1)
            pool.affine_select(out=group[:, :], in_=group[:, :], compare_op=ALU.is_ge, fill=0.0, base=0,
                               pattern=[[-4, 32], [0, 4]], channel_multiplier=1).then_inc(consts_made, 1)
            pool.affine_select(out=lower[:, :, :], in_=lower[:, :, :], compare_op=ALU.is_gt, fill=0.0, base=0,
                               pattern=[[1, E], [-1, E]], channel_multiplier=0).then_inc(consts_made, 1)
            pool.wait_ge(consts_made, 8)
            pool.affine_select(out=group[:, :], in_=group[:, :], compare_op=ALU.is_ge, fill=0.0, base=3,
                               pattern=[[4, 32], [0, 4]], channel_multiplier=-1).then_inc(consts_made, 1)
            pool.wait_ge(consts_made, 9)
            with pool.Fori(0, B) as b:
                for step in PLAN:
                    kind = step[0]
                    if kind == "gn":
                        pool.wait_ge(gn_var_ready, at(pool, b, gn_var_ready, *step))
                        pool.tensor_tensor(grstd, gve, minus_half[:, 0:1], ALU.pow).then_inc(gn_rstd_ready, 1)
                    if kind == "ln":
                        pool.wait_ge(ln_var_ready, at(pool, b, ln_var_ready, *step))
                        pool.tensor_tensor(ln_rs[:, :], ln_ve[:, :], minus_half[:, :], ALU.pow)\
                            .then_inc(ln_rstd_ready, 1)
                    if kind == "uln":
                        pool.wait_ge(u_var_ready, at(pool, b, u_var_ready, *step))
                        pool.tensor_tensor(u_rs[:, :], u_ve[:, :], minus_half[:, :], ALU.pow)\
                            .then_inc(u_rstd_ready, 1)

        @block.scalar
        def _(act):
            act.sem_inc(o1_chan_ready, 1)
            act.sem_inc(p1_exp_ready, 1)
            act.sem_inc(p1_hi_ready, 1)
            act.sem_inc(y_chan_ready, 1)
            act.wait_ge(w_split, W_SPLITS)

            with act.Fori(0, B) as b:
                for step in PLAN:
                    kind = step[0]
                    if kind == "gn":
                        act.wait_ge(ring_full, filled(act, b, step, 3))
                        act.activation(se_e, ps[:, RING0 + ring_index(step, 3) % 2, 0:1], ACT.Exp, scale=-1.0)\
                            .then_inc(se_exp_ready, 1)
                    elif kind == "xg":
                        u = step[1]
                        act.wait_ge(xg_norm_ready, at(act, b, xg_norm_ready, *step))
                        act.activation(xt_hi[:, u * LW:(u + 1) * LW], xg_f[:, u % 2, :], ACT.Copy)\
                            .then_inc(xg_hi_ready, 1)
                    elif kind == "kproj":
                        m = step[1]
                        act.wait_ge(ring_full, filled(act, b, step))
                        act.activation(k_hi[:, m * BW:(m + 1) * BW], ring_bank(step)[:, 0:BW], ACT.Identity,
                                       bias=biases[:, 1:2]).then_inc(k_hi_ready, 1)
                    elif kind == "vproj":
                        m = step[1]
                        act.wait_ge(ring_full, filled(act, b, step))
                        if m >= 2:
                            act.wait_ge(ring_full, filled(act, b, ("vt", m - 2)))
                        act.activation(v_chan[:, m % 2, :], ring_bank(step)[:, 0:BW], ACT.Identity,
                                       bias=biases[:, 2:3]).then_inc(v_chan_ready, 1)
                    elif kind == "vt":
                        m = step[1]
                        act.wait_ge(ring_full, filled(act, b, step))
                        act.activation(v_hi[:, TPB * m:TPB * (m + 1), :], tiled(ring_bank(step)[:, 0:BW]), ACT.Copy)\
                            .then_inc(v_hi_ready, 1)
                    elif kind == "baset":
                        m = step[1]
                        act.wait_ge(ring_full, filled(act, b, step))
                        act.activation(t_tok[:, TPB * m:TPB * (m + 1), :], tiled(ring_bank(step)[:, 0:BW]), ACT.Copy)\
                            .then_inc(base_tok_ready, 1)
                    elif kind == "qproj":
                        n = step[1]
                        act.wait_ge(ring_full, filled(act, b, step))
                        act.activation(q_hi[:, n % 2, :], ring_bank(step)[:, 0:BW], ACT.Identity,
                                       bias=biases[:, 0:1]).then_inc(q_hi_ready, 1)
                    elif kind == "exp":
                        n, r, c = step[1:]
                        a, w = QC[c]
                        if c == 0:
                            act.wait_ge(row_max_ready, at(act, b, row_max_ready, "scores", n, r, 2))
                            if r == 0 and n >= 2:
                                act.wait_ge(ring_full, filled(act, b, ("pt", n - 2, NT - 1)))
                            if r == 0 and n == 0:
                                act.wait_ge(ring_full, before(act, b, ring_full))
                                act.wait_ge(p1_lo_ready, before(act, b, p1_lo_ready))
                                act.wait_ge(o_added, before(act, b, o_added))
                        banks = ps[:, 2 * c:2 * c + 2, :] if c < 2 else ps[:, 4, 0:w]
                        out = p_rows[:, n % 2, r, a:a + w]
                        if c < 2:
                            out = out.rearrange("p (s w) -> p s w", w=512)
                        act.activation(out, banks, ACT.Exp, bias=negmax[:, r % 2:r % 2 + 1],
                                       accum_out=dparts[:, n, r, c:c + 1]).then_inc(p_rows_ready, 1)
                    elif kind == "pt":
                        n, j = step[1:]
                        g = n * NT + j
                        slot = g % PTS
                        act.wait_ge(ring_full, filled(act, b, step))
                        if g >= PTS:
                            act.wait_ge(pv_done, at(act, b, pv_done, "pv", (g - PTS) // NT, (g - PTS) % NT))
                        else:
                            act.wait_ge(pv1_done, before(act, b, pv1_done))
                        act.activation(pt_hi[:, slot, :], ring_bank(step)[:, 0:BW], ACT.Copy)\
                            .then_inc(pt_hi_ready, 1)
                    elif kind == "oevac":
                        m = step[1]
                        act.wait_ge(pv_done, at(act, b, pv_done, "pv", m, NT - 1))
                        if m >= 1:
                            act.wait_ge(ring_full, filled(act, b, ("ot", m - 1)))
                        act.activation(o_chan[:, :], ps[:, 5, 0:BW], ACT.Copy).then_inc(o_chan_ready, 1)
                    elif kind == "lnapply":
                        m = step[1]
                        act.wait_ge(tn_tok_ready, at(act, b, tn_tok_ready, *step))
                        if m == 0:
                            act.wait_ge(pv1_done, before(act, b, pv1_done))
                        act.activation(tn_hi[:, TPB * m:TPB * (m + 1), :], tn_tok[:, :, :], ACT.Copy)\
                            .then_inc(tn_hi_ready, 1)
                    elif kind == "tnt":
                        m = step[1]
                        act.wait_ge(ring_full, filled(act, b, step))
                        act.activation(xt_hi[:, m * BW:(m + 1) * BW], ring_bank(step)[:, 0:BW], ACT.Copy)\
                            .then_inc(tnt_hi_ready, 1)
                    elif kind == "s1":
                        w = step[1]
                        ib, j = divmod(w, NT)
                        act.wait_ge(s1_done, at(act, b, s1_done, *step))
                        if w == 0:
                            act.wait_ge(r1_done, before(act, b, r1_done))
                            act.wait_ge(ring_full, filled(act, b, ("pt", NB - 1, NT - 1)))
                        if w >= 2:
                            act.wait_ge(p1_lo_ready, at(act, b, p1_lo_ready, "s1", w - 2))
                        act.activation(p1_f[:, w % 2, :].rearrange("p (s w) -> p s w", s=2),
                                       ps[:, 2 * (w % 2):2 * (w % 2) + 2, 0:BW], ACT.Exp, bias=shift[:, :],
                                       accum_out=d1parts[:, j, ib:ib + 1]).then_inc(p1_exp_ready, 1)
                        if w >= 3:
                            act.wait_ge(pv1_done, at(act, b, pv1_done, "pv1", w - 3))
                        else:
                            act.wait_ge(pv_done, at(act, b, pv_done, "pv", NB - 1, NT - 1))
                        act.wait_ge(p1_exp_ready, at(act, b, p1_exp_ready, *step))
                        act.activation(p1_hi[:, w % 3, :], p1_f[:, w % 2, :], ACT.Copy).then_inc(p1_hi_ready, 1)
                    elif kind == "o1evac":
                        ib = step[1]
                        act.wait_ge(pv1_done, at(act, b, pv1_done, "pv1", ib * NT + NT - 1))
                        dst = o1_chan[:, ib * LW:(ib + 1) * LW].rearrange("p (s w) -> p s w", s=2)
                        act.activation(dst, ps[:, 4:6, 0:BW], ACT.Copy).then_inc(o1_chan_ready, 1)
                    elif kind == "ut":
                        act.wait_ge(ring_full, filled(act, b, step))
                        act.activation(u_hi[:, :], ring_bank(step)[:, 0:BW], ACT.Copy).then_inc(u_hi_ready, 1)
                    elif kind == "router":
                        act.wait_ge(logit_max_ready, at(act, b, logit_max_ready, *step))
                        act.activation(gexp[:, :, :], centred[:, :, :], ACT.Exp).then_inc(gate_exp_ready, 1)
                    elif kind == "yt":
                        mb = step[1]
                        act.wait_ge(ring_full, filled(act, b, step))
                        act.wait_ge(y_stored[mb % 2], value(act, b, 16 * (NB // 2), 16 * (mb // 2) + 1))
                        act.activation(y_out[:, mb % 2, :], ring_bank(step)[:, 0:BW], ACT.Copy)\
                            .then_inc(y_chan_ready, 1)

        @block.vector
        def _(dve):
            dve.sem_inc(expert_added, 1)
            dve.sem_inc(o_added, 1)
            dve.sem_inc(p1_lo_ready, 1)
            dve.sem_inc(r1_done, 1)
            dve.memset(eb_stage, 0.0).then_inc(eb_zeroed, 1)
            dve.wait_ge(w_loaded, 16 * (N_WLOADS + 2))
            dve.tensor_copy(w_hi[:, :, :], w_stage).then_inc(w_split, 1)
            dve.tensor_copy(rw_hi[:, :], rw_stage).then_inc(w_split, 1)
            dve.tensor_copy(ew_hi[:, :], ew_stage).then_inc(w_split, 1)
            dve.tensor_copy(eb_rows[:, :], eb_stage).then_inc(w_split, 1)
            dve.wait_ge(w_split, 4)
            dve.tensor_tensor(w_lo[:, :, :], w_stage, w_hi[:, :, :], ALU.subtract).then_inc(w_split, 1)
            dve.tensor_tensor(rw_lo[:, :], rw_stage, rw_hi[:, :], ALU.subtract).then_inc(w_split, 1)
            dve.tensor_tensor(ew_lo[:, :], ew_stage, ew_hi[:, :], ALU.subtract).then_inc(w_split, 1)
            dve.tensor_tensor(eb_rows[32:64, :], eb_stage[32:64, :], eb_rows[32:64, :], ALU.subtract)\
                .then_inc(w_split, 1)
            dve.memset(eb_split[:, 0:128], 1.0).then_inc(eb_zeroed, 1)
            dve.wait_ge(eb_zeroed, 2)
            dve.tensor_copy(ones[:, :], eb_split[:, 0:128]).then_inc(w_split, 1)
            dve.wait_ge(w_split, W_SPLITS)
            dve.wait_ge(consts_made, 9)

            with dve.Fori(0, B) as b:
                for step in PLAN:
                    kind = step[0]
                    links = [0]

                    def link(ins):
                        links[0] += 1
                        ins.then_inc(vector_chain, 1)

                    if kind == "gn":
                        dve.wait_ge(x_loaded, value(dve, b, 16, 16))
                        for m in range(NB):
                            link(dve.bn_stats(gn_raw[:, m, :], x_chan[:, m * BW:(m + 1) * BW]))
                        dve.wait_ge(vector_chain, chained(b, step, links[0]))
                        dve.memset(wait_carrier[:, :], 0.0)
                        dve.bn_aggr(gn_mv[:, :], gn_raw[:, :, :]).then_inc(gn_stats_ready, 1)
                        dve.wait_ge(gn_stats_ready, at(dve, b, gn_stats_ready, *step))
                        dve.wait_ge(ring_full, filled(dve, b, step, 0))
                        bank = ps[:, RING0 + ring_index(step, 0) % 2, 0:1]
                        link(dve.tensor_copy(gmean, bank))
                        link(dve.tensor_tensor(gdev, gn_mv[:, 0:1], bank, ALU.subtract))
                        dve.wait_ge(vector_chain, chained(b, step, links[0]))
                        dve.scalar_tensor_tensor(out=gsq, in0=gdev, scalar=gdev, in1=gn_mv[:, 1:2], op0=ALU.mult,
                                                 op1=ALU.add).then_inc(gn_dev_ready, 1)
                        dve.wait_ge(ring_full, filled(dve, b, step, 1))
                        dve.tensor_scalar(gve, ps[:, RING0 + ring_index(step, 1) % 2, 0:1], GN_EPS, None, ALU.add)\
                            .then_inc(gn_var_ready, 1)
                        dve.wait_ge(gn_rstd_ready, at(dve, b, gn_rstd_ready, *step))
                        dve.tensor_tensor(se_in, gdev, grstd, ALU.mult).then_inc(se_in_ready, 1)
                        dve.wait_ge(ring_full, filled(dve, b, step, 2))
                        dve.tensor_scalar(se_h[0:RED, :], ps[0:RED, RING0 + ring_index(step, 2) % 2, 0:1], 0.0, None,
                                          ALU.max).then_inc(se_hidden_ready, 1)
                        dve.wait_ge(se_exp_ready, at(dve, b, se_exp_ready, *step))
                        link(dve.tensor_scalar(se_tmp, se_e, 1.0, None, ALU.add))
                        dve.wait_ge(vector_chain, chained(b, step, links[0]))
                        link(dve.reciprocal(ysig, se_tmp))
                        dve.wait_ge(vector_chain, chained(b, step, links[0]))
                        link(dve.tensor_tensor(ysig, ysig, grstd, ALU.mult))
                        dve.wait_ge(vector_chain, chained(b, step, links[0]))
                        link(dve.tensor_scalar(yscale, ysig, 1.0, None, ALU.add))
                        link(dve.scalar_tensor_tensor(out=yshift, in0=gmean, scalar=-1.0, in1=ysig, op0=ALU.mult,
                                                      op1=ALU.mult))
                        dve.wait_ge(vector_chain, chained(b, step, links[0]))
                    elif kind == "xg":
                        u = step[1]
                        if u == 0:
                            dve.wait_ge(ring_full, before(dve, b, ring_full))
                            dve.wait_ge(p1_lo_ready, before(dve, b, p1_lo_ready))
                            dve.wait_ge(p1_hi_ready, before(dve, b, p1_hi_ready))
                        else:
                            dve.wait_ge(xg_norm_ready, at(dve, b, xg_norm_ready, "xg", u - 1))
                        if u >= 2:
                            dve.wait_ge(xg_lo_ready, at(dve, b, xg_lo_ready, "xg", u - 2))
                        dve.tensor_scalar(xg_f[:, u % 2, :], x_chan[:, u * LW:(u + 1) * LW], gmean, grstd,
                                          ALU.subtract, ALU.mult).then_inc(xg_norm_ready, 1)
                        dve.wait_ge(xg_norm_ready, at(dve, b, xg_norm_ready, *step))
                        dve.wait_ge(xg_hi_ready, at(dve, b, xg_hi_ready, *step))
                        dve.tensor_tensor(xt_lo[:, u * LW:(u + 1) * LW], xg_f[:, u % 2, :],
                                          xt_hi[:, u * LW:(u + 1) * LW], ALU.subtract).then_inc(xg_lo_ready, 1)
                    elif kind == "base":
                        dve.wait_ge(xg_lo_ready, at(dve, b, xg_lo_ready, "xg", 2))
                        dve.tensor_scalar(x_chan[:, :], x_chan[:, :], yscale, yshift, ALU.mult, ALU.add)\
                            .then_inc(base_done, 1)
                    elif kind == "kproj":
                        m = step[1]
                        dve.wait_ge(k_hi_ready, at(dve, b, k_hi_ready, *step))
                        dve.scalar_tensor_tensor(out=k_lo[:, m * BW:(m + 1) * BW], in0=ring_bank(step)[:, 0:BW],
                                                 scalar=biases[:, 1:2], in1=k_hi[:, m * BW:(m + 1) * BW], op0=ALU.add,
                                                 op1=ALU.subtract).then_inc(k_lo_ready, 1)
                    elif kind == "qproj":
                        n = step[1]
                        dve.wait_ge(q_hi_ready, at(dve, b, q_hi_ready, *step))
                        dve.scalar_tensor_tensor(out=q_lo[:, n % 2, :], in0=ring_bank(step)[:, 0:BW],
                                                 scalar=biases[:, 0:1], in1=q_hi[:, n % 2, :], op0=ALU.add,
                                                 op1=ALU.subtract).then_inc(q_lo_ready, 1)
                    elif kind == "vt":
                        m = step[1]
                        dve.wait_ge(v_hi_ready, at(dve, b, v_hi_ready, *step))
                        dve.tensor_tensor(v_lo[:, TPB * m:TPB * (m + 1), :], tiled(ring_bank(step)[:, 0:BW]),
                                          v_hi[:, TPB * m:TPB * (m + 1), :], ALU.subtract).then_inc(v_lo_ready, 1)
                    elif kind == "scores":
                        n, r, q = step[1:]
                        dve.wait_ge(scores_done, at(dve, b, scores_done, *step))
                        banks = ps[:, 2 * q:2 * q + 2, :] if q < 2 else ps[:, 4, 0:QC[2][1]]
                        link(dve.tensor_reduce(mx[:, q:q + 1], banks, AX.XY if q < 2 else AX.X, ALU.max))
                        dve.wait_ge(vector_chain, chained(b, step, links[0]))
                        dve.tensor_reduce(negmax[:, r % 2:r % 2 + 1], mx[:, 0:q + 1], AX.X, ALU.max, negate=True)\
                            .then_inc(row_max_ready, 1)
                    elif kind == "pt":
                        n, j = step[1:]
                        slot = (n * NT + j) % PTS
                        dve.wait_ge(pt_hi_ready, at(dve, b, pt_hi_ready, *step))
                        dve.tensor_tensor(pt_lo[:, slot, :], ring_bank(step)[:, 0:BW], pt_hi[:, slot, :],
                                          ALU.subtract).then_inc(pt_lo_ready, 1)
                    elif kind == "ot":
                        m = step[1]
                        dve.wait_ge(p_rows_ready, at(dve, b, p_rows_ready, "exp", m, TPB - 1, 2))
                        link(dve.tensor_reduce(rg[:, 0, :], dparts[:, m, :, :], AX.X, ALU.add))
                        dve.wait_ge(vector_chain, chained(b, step, links[0]))
                        link(dve.reciprocal(rg[:, 1, :], rg[:, 0, :]))
                        dve.wait_ge(vector_chain, chained(b, step, links[0]))
                        link(dve.tensor_scalar(rg[:, 2, :], rg[:, 1, :], biases[:, 3:4], None, ALU.mult))
                        dve.wait_ge(vector_chain, chained(b, step, links[0]))
                        dve.wait_ge(ring_full, filled(dve, b, step))
                        dve.wait_ge(base_tok_ready, at(dve, b, base_tok_ready, "baset", m))
                        for k in range(TPB):
                            t = t_tok[:, TPB * m + k, :]
                            ins = dve.scalar_tensor_tensor(out=t, in0=ring_bank(step)[:, k * 128:(k + 1) * 128],
                                                           scalar=rg[:, 2, k:k + 1], in1=t, op0=ALU.mult, op1=ALU.add)
                            if k < TPB - 1:
                                link(ins)
                        ins.then_inc(o_added, 1)
                    elif kind in ("ln", "uln"):
                        m = step[1]
                        raw, mv, ve = (ln_raw, ln_mv, ln_ve) if kind == "ln" else (u_raw, u_mv, u_ve)
                        src = t_tok
                        if kind == "ln":
                            dve.wait_ge(o_added, at(dve, b, o_added, "ot", m))
                        else:
                            dve.wait_ge(o1_added, at(dve, b, o1_added, "o1t", m))
                        for k in range(TPB):
                            link(dve.bn_stats(raw[:, k, :], src[:, TPB * m + k, :]))
                        dve.wait_ge(vector_chain, chained(b, step, links[0]))
                        dve.memset(wait_carrier[:, :], 0.0)
                        for k in range(TPB):
                            link(dve.bn_aggr(mv[:, k, :], raw[:, k, :]))
                        dve.wait_ge(vector_chain, chained(b, step, links[0]))
                        dve.tensor_scalar(ve[:, :], mv[:, :, 1], LN_EPS, None, ALU.add)\
                            .then_inc(ln_var_ready if kind == "ln" else u_var_ready, 1)
                    elif kind in ("lnapply", "uapply"):
                        m = step[1]
                        mv, rs, dst = (ln_mv, ln_rs, tn_tok) if kind == "lnapply" else (u_mv, u_rs, u_tok)
                        if kind == "lnapply":
                            dve.wait_ge(ln_rstd_ready, at(dve, b, ln_rstd_ready, "ln", m))
                        else:
                            dve.wait_ge(u_rstd_ready, at(dve, b, u_rstd_ready, "uln", m))
                        if m >= 1:
                            dve.wait_ge(ring_full, filled(dve, b, ("tnt" if kind == "lnapply" else "ut", m - 1)))
                        for k in range(TPB):
                            ins = dve.tensor_scalar(dst[:, k, :], t_tok[:, TPB * m + k, :], mv[:, k, 0:1],
                                                    rs[:, k:k + 1], ALU.subtract, ALU.mult)
                            if k < TPB - 1:
                                link(ins)
                        if kind == "uapply":
                            ins.then_inc(u_tok_ready, 1)
                            continue
                        ins.then_inc(tn_tok_ready, 1)
                        dve.wait_ge(tn_hi_ready, at(dve, b, tn_hi_ready, *step))
                        dve.tensor_tensor(tn_lo[:, TPB * m:TPB * (m + 1), :], tn_tok[:, :, :],
                                          tn_hi[:, TPB * m:TPB * (m + 1), :], ALU.subtract).then_inc(tn_lo_ready, 1)
                    elif kind == "tnt":
                        m = step[1]
                        dve.wait_ge(tnt_hi_ready, at(dve, b, tnt_hi_ready, *step))
                        dve.tensor_tensor(xt_lo[:, m * BW:(m + 1) * BW], ring_bank(step)[:, 0:BW],
                                          xt_hi[:, m * BW:(m + 1) * BW], ALU.subtract).then_inc(tnt_lo_ready, 1)
                    elif kind == "s1":
                        w = step[1]
                        dve.wait_ge(p1_hi_ready, at(dve, b, p1_hi_ready, *step))
                        dve.tensor_tensor(p1_lo[:, w % 3, :], p1_f[:, w % 2, :], p1_hi[:, w % 3, :],
                                          ALU.subtract).then_inc(p1_lo_ready, 1)
                    elif kind == "rd1":
                        dve.wait_ge(p1_exp_ready, at(dve, b, p1_exp_ready, "s1", LB * NT - 1))
                        link(dve.tensor_reduce(r1[:, 0, :], d1parts[:, :, :], AX.X, ALU.add))
                        dve.wait_ge(vector_chain, chained(b, step, links[0]))
                        dve.reciprocal(r1[:, 1, :], r1[:, 0, :]).then_inc(r1_done, 1)
                        dve.wait_ge(r1_done, at(dve, b, r1_done, *step))
                    elif kind == "o1t":
                        m = step[1]
                        dve.wait_ge(ring_full, filled(dve, b, step))
                        for k in range(TPB):
                            t = t_tok[:, TPB * m + k, :]
                            ins = dve.scalar_tensor_tensor(out=t, in0=ring_bank(step)[:, k * 128:(k + 1) * 128],
                                                           scalar=r1[:, 1, TPB * m + k:TPB * m + k + 1], in1=t,
                                                           op0=ALU.mult, op1=ALU.add)
                            if k < TPB - 1:
                                link(ins)
                        ins.then_inc(o1_added, 1)
                    elif kind == "ut":
                        dve.wait_ge(u_hi_ready, at(dve, b, u_hi_ready, *step))
                        dve.tensor_tensor(u_lo[:, :], ring_bank(step)[:, 0:BW], u_hi[:, :],
                                          ALU.subtract).then_inc(u_lo_ready, 1)
                    elif kind == "router":
                        m = step[1]
                        dve.wait_ge(ring_full, filled(dve, b, step))
                        shape = [128, TPB, E]
                        link(dve.tensor_tensor(logits[:, :, :],
                                               ring_bank(step)[:, 0:TPB * E].rearrange("p (t e) -> p t e", e=E),
                                               rb_sb[:, :].unsqueeze(1).broadcast_to(shape), ALU.add))
                        dve.wait_ge(vector_chain, chained(b, step, links[0]))
                        link(dve.tensor_reduce(lmax[:, :], logits[:, :, :], AX.X, ALU.max))
                        dve.wait_ge(vector_chain, chained(b, step, links[0]))
                        dve.tensor_tensor(centred[:, :, :], logits[:, :, :],
                                          lmax[:, :].unsqueeze(2).broadcast_to(shape),
                                          ALU.subtract).then_inc(logit_max_ready, 1)
                        own = logits[:, :, :].unsqueeze(3).broadcast_to([128, TPB, E, E])
                        other = logits[:, :, :].unsqueeze(2).broadcast_to([128, TPB, E, E])
                        low = lower[:, :, :].unsqueeze(1).broadcast_to([128, TPB, E, E])
                        link(dve.tensor_tensor(cmp_gt[:, :, :, :], other, own, ALU.is_gt))
                        link(dve.tensor_tensor(cmp_ge[:, :, :, :], other, own, ALU.is_ge))
                        dve.wait_ge(vector_chain, chained(b, step, links[0]))
                        link(dve.tensor_tensor(cmp_ge[:, :, :, :], cmp_ge[:, :, :, :], low, ALU.mult))
                        dve.wait_ge(vector_chain, chained(b, step, links[0]))
                        link(dve.tensor_tensor(cmp_gt[:, :, :, :], cmp_ge[:, :, :, :], cmp_gt[:, :, :, :], ALU.max))
                        dve.wait_ge(vector_chain, chained(b, step, links[0]))
                        link(dve.tensor_reduce(rank[:, :, :], cmp_gt[:, :, :, :], AX.X, ALU.add))
                        dve.wait_ge(vector_chain, chained(b, step, links[0]))
                        link(dve.tensor_scalar(rank[:, :, :], rank[:, :, :], 2.0, None, ALU.is_lt))
                        dve.wait_ge(vector_chain, chained(b, step, links[0]))
                        dve.wait_ge(gate_exp_ready, at(dve, b, gate_exp_ready, *step))
                        link(dve.tensor_tensor(gexp[:, :, :], gexp[:, :, :], rank[:, :, :], ALU.mult))
                        dve.wait_ge(vector_chain, chained(b, step, links[0]))
                        link(dve.tensor_reduce(gsum[:, 0, :], gexp[:, :, :], AX.X, ALU.add))
                        dve.wait_ge(vector_chain, chained(b, step, links[0]))
                        link(dve.reciprocal(gsum[:, 1, :], gsum[:, 0, :]))
                        dve.wait_ge(vector_chain, chained(b, step, links[0]))
                        dve.tensor_tensor(gates[:, m % 2, :, :], gexp[:, :, :],
                                          gsum[:, 1, :].unsqueeze(2).broadcast_to(shape),
                                          ALU.mult).then_inc(gates_ready, 1)
                    elif kind == "expert":
                        m, k, half = step[1:]
                        dve.wait_ge(ring_full, filled(dve, b, step))
                        if half == 0 and k == 0:
                            dve.wait_ge(gates_ready, at(dve, b, gates_ready, "router", m))
                            if m >= 2:
                                dve.wait_ge(ring_full, filled(dve, b, ("yt", m - 2)))
                        if half == 1:
                            dve.wait_ge(expert_added, at(dve, b, expert_added, "expert", m, k, 0))
                        for e in range(E // 2):
                            src = t_tok[:, TPB * m + k, :] if half == 0 and e == 0 else acc[:, m % 2, k, :]
                            ins = dve.scalar_tensor_tensor(
                                out=acc[:, m % 2, k, :], in0=ring_bank(step)[:, e * 128:(e + 1) * 128],
                                scalar=gates[:, m % 2, k, half * 4 + e:half * 4 + e + 1], in1=src,
                                op0=ALU.mult, op1=ALU.add)
                            if e < E // 2 - 1:
                                link(ins)
                                dve.wait_ge(vector_chain, chained(b, step, links[0]))
                        ins.then_inc(expert_added, 1)
                    assert links[0] == CHAINED.get(kind, 0), (kind, links[0])

        @block.tensor
        def _(pe):
            pe.sem_inc(pv1_done, 1)
            pe.sem_inc(ring_full, 1)
            pe.wait_ge(w_split, W_SPLITS)
            pe.wait_ge(consts_made, 9)

            def three(out, lhs_hi, lhs_lo, rhs_hi, rhs_lo, start=True, stop=True):
                pe.matmul(out, lhs_hi, rhs_hi, start=start, stop=False)
                pe.matmul(out, lhs_hi, rhs_lo, start=False, stop=False)
                return pe.matmul(out, lhs_lo, rhs_hi, start=False, stop=stop)

            def transpose3(b, step, src):
                pe.wait_ge(reader(step), freed(pe, b, step))
                for k in range(TPB):
                    ins = pe.transpose(ring_bank(step)[:, k * 128:(k + 1) * 128], src(k), ident[:, :])
                ins.then_inc(ring_full, 1)

            def project(b, step, w):
                m = step[1]
                pe.wait_ge(reader(step), freed(pe, b, step))
                cols = slice(m * BW, (m + 1) * BW)
                three(ring_bank(step)[:, 0:BW], w_hi[:, w, :], w_lo[:, w, :], xt_hi[:, cols], xt_lo[:, cols])\
                    .then_inc(ring_full, 1)

            with pe.Fori(0, B) as b:
                for step in PLAN:
                    kind = step[0]
                    if kind == "gn":
                        col = [ps[:, RING0 + ring_index(step, i) % 2, 0:1] for i in range(4)]
                        pe.wait_ge(reader(step, 0), freed(pe, b, step, 0))
                        pe.wait_ge(gn_stats_ready, at(pe, b, gn_stats_ready, *step))
                        pe.matmul(col[0], group[:, :], gn_mv[:, 0:1], start=True, stop=True)\
                            .then_inc(ring_full, 1)
                        pe.wait_ge(reader(step, 1), freed(pe, b, step, 1))
                        pe.wait_ge(gn_dev_ready, at(pe, b, gn_dev_ready, *step))
                        pe.matmul(col[1], group[:, :], gsq, start=True, stop=True).then_inc(ring_full, 1)
                        pe.wait_ge(se_in_ready, at(pe, b, se_in_ready, *step))
                        pe.matmul(col[2][0:RED, :], w1_sb[:, :], se_in, start=True, stop=True)\
                            .then_inc(ring_full, 1)
                        pe.wait_ge(se_hidden_ready, at(pe, b, se_hidden_ready, *step))
                        pe.matmul(col[3], w2_sb[:, :], se_h[0:RED, :], start=True, stop=True)\
                            .then_inc(ring_full, 1)
                    elif kind in ("kproj", "vproj", "qproj"):
                        pe.wait_ge(xg_lo_ready, at(pe, b, xg_lo_ready, "xg", step[1] // 2))
                        project(b, step, {"qproj": 0, "kproj": 1, "vproj": 2}[kind])
                    elif kind == "vt":
                        m = step[1]
                        pe.wait_ge(v_chan_ready, at(pe, b, v_chan_ready, "vproj", m))
                        transpose3(b, step, lambda k: v_chan[:, m % 2, k * 128:(k + 1) * 128])
                    elif kind == "baset":
                        m = step[1]
                        pe.wait_ge(base_done, at(pe, b, base_done, "base"))
                        transpose3(b, step, lambda k: x_chan[:, m * BW + k * 128:m * BW + (k + 1) * 128])
                    elif kind == "scores":
                        n, r, q = step[1:]
                        if q == 0:
                            pe.wait_ge(q_lo_ready, at(pe, b, q_lo_ready, "qproj", n))
                            if n == 0 and r == 0:
                                pe.wait_ge(k_lo_ready, at(pe, b, k_lo_ready, "kproj", NB - 1))
                        row = n * TPB + r
                        if row:
                            pe.wait_ge(p_rows_ready, at(pe, b, p_rows_ready, "exp", (row - 1) // TPB, (row - 1) % TPB, q))
                        elif q < 2:
                            pe.wait_ge(p1_exp_ready, before(pe, b, p1_exp_ready))
                        else:
                            pe.wait_ge(o1_chan_ready, before(pe, b, o1_chan_ready))
                        a, w = QC[q]
                        for i in range(-(-w // 512)):
                            cols = slice(a + i * 512, min(a + i * 512 + 512, a + w))
                            tile = slice(r * 128, (r + 1) * 128)
                            ins = three(ps[:, 2 * q + i, 0:cols.stop - cols.start], q_hi[:, n % 2, tile],
                                        q_lo[:, n % 2, tile], k_hi[:, cols], k_lo[:, cols])
                        ins.then_inc(scores_done, 1)
                    elif kind == "pt":
                        n, j = step[1:]
                        pe.wait_ge(p_rows_ready, at(pe, b, p_rows_ready, "exp", n, TPB - 1, chunk_of(j)))
                        transpose3(b, step, lambda k: p_rows[:, n % 2, k, j * 128:(j + 1) * 128])
                    elif kind == "pv":
                        n, j = step[1:]
                        slot = (n * NT + j) % PTS
                        pe.wait_ge(pt_lo_ready, at(pe, b, pt_lo_ready, "pt", n, j))
                        if j == 0:
                            if n:
                                pe.wait_ge(o_chan_ready, at(pe, b, o_chan_ready, "oevac", n - 1))
                            else:
                                pe.wait_ge(v_lo_ready, at(pe, b, v_lo_ready, "vt", NB - 1))
                                pe.wait_ge(o1_chan_ready, before(pe, b, o1_chan_ready))
                        three(ps[:, 5, 0:BW], v_hi[:, j, :], v_lo[:, j, :], pt_hi[:, slot, :], pt_lo[:, slot, :],
                              start=j == 0, stop=j == NT - 1).then_inc(pv_done, 1)
                    elif kind == "ot":
                        pe.wait_ge(o_chan_ready, at(pe, b, o_chan_ready, "oevac", step[1]))
                        transpose3(b, step, lambda k: o_chan[:, k * 128:(k + 1) * 128])
                    elif kind == "tnt":
                        pe.wait_ge(tn_tok_ready, at(pe, b, tn_tok_ready, "lnapply", step[1]))
                        transpose3(b, step, lambda k: tn_tok[:, k, :])
                    elif kind == "s1":
                        w = step[1]
                        ib, j = divmod(w, NT)
                        if ib == 0:
                            pe.wait_ge(tnt_lo_ready, at(pe, b, tnt_lo_ready, "tnt", max(j // TPB, 1)))
                        if w >= 2:
                            pe.wait_ge(p1_exp_ready, at(pe, b, p1_exp_ready, "s1", w - 2))
                        else:
                            pe.wait_ge(p_rows_ready, at(pe, b, p_rows_ready, "exp", NB - 1, TPB - 1, 1))
                        tile = slice(j * 128, (j + 1) * 128)
                        for i in range(2):
                            cols = slice(ib * LW + i * BW, ib * LW + (i + 1) * BW)
                            ins = three(ps[:, 2 * (w % 2) + i, 0:BW], xt_hi[:, tile], xt_lo[:, tile], xt_hi[:, cols],
                                        xt_lo[:, cols])
                        ins.then_inc(s1_done, 1)
                    elif kind == "pv1":
                        w = step[1]
                        ib, j = divmod(w, NT)
                        pe.wait_ge(p1_lo_ready, at(pe, b, p1_lo_ready, "s1", w))
                        if ib == 0:
                            pe.wait_ge(tn_lo_ready, at(pe, b, tn_lo_ready, "lnapply", j // TPB))
                        if j == 0:
                            if ib:
                                pe.wait_ge(o1_chan_ready, at(pe, b, o1_chan_ready, "o1evac", ib - 1))
                            else:
                                pe.wait_ge(o_chan_ready, at(pe, b, o_chan_ready, "oevac", NB - 1))
                                pe.wait_ge(p_rows_ready, at(pe, b, p_rows_ready, "exp", NB - 1, TPB - 1, 2))
                        for i in range(2):
                            cols = slice(i * BW, (i + 1) * BW)
                            ins = three(ps[:, 4 + i, 0:BW], tn_hi[:, j, :], tn_lo[:, j, :],
                                        p1_hi[:, w % 3, cols], p1_lo[:, w % 3, cols], start=j == 0, stop=j == NT - 1)
                        ins.then_inc(pv1_done, 1)
                    elif kind == "o1t":
                        m = step[1]
                        pe.wait_ge(o1_chan_ready, at(pe, b, o1_chan_ready, "o1evac", m // 2))
                        transpose3(b, step, lambda k: o1_chan[:, m * BW + k * 128:m * BW + (k + 1) * 128])
                    elif kind == "ut":
                        pe.wait_ge(u_tok_ready, at(pe, b, u_tok_ready, "uapply", step[1]))
                        transpose3(b, step, lambda k: u_tok[:, k, :])
                    elif kind == "router":
                        m = step[1]
                        pe.wait_ge(u_lo_ready, at(pe, b, u_lo_ready, "ut", m))
                        pe.wait_ge(reader(step), freed(pe, b, step))
                        for k in range(TPB):
                            tile = slice(k * 128, (k + 1) * 128)
                            out = ring_bank(step)[:, k * E:(k + 1) * E]
                            pe.matmul(out, u_lo[:, tile], rw_lo[:, :], start=True, stop=False)
                            pe.matmul(out, u_hi[:, tile], rw_lo[:, :], start=False, stop=False)
                            pe.matmul(out, u_lo[:, tile], rw_hi[:, :], start=False, stop=False)
                            ins = pe.matmul(out, u_hi[:, tile], rw_hi[:, :], start=False, stop=True)
                        ins.then_inc(ring_full, 1)
                    elif kind == "expert":
                        m, k, half = step[1:]
                        pe.wait_ge(reader(step), freed(pe, b, step))
                        tile = slice(k * 128, (k + 1) * 128)
                        cols = slice(half * 512, (half + 1) * 512)
                        out = ring_bank(step)
                        pe.matmul(out, ones[0:64, :], eb_rows[0:64, cols], start=True, stop=False)
                        three(out, u_hi[:, tile], u_lo[:, tile], ew_hi[:, cols], ew_lo[:, cols], start=False)\
                            .then_inc(ring_full, 1)
                    elif kind == "yt":
                        m = step[1]
                        pe.wait_ge(expert_added, at(pe, b, expert_added, "expert", m, TPB - 1, 1))
                        transpose3(b, step, lambda k: acc[:, m % 2, k, :])


_INS = ["x", "wq", "wk", "wv", "bq", "bk", "bv", "w1", "w2", "gamma", "rw", "rb", "ew", "eb"]


def kernel(x, L0_conv_Wq, L0_conv_bq, L0_conv_Wk, L0_conv_bk, L0_conv_Wv, L0_conv_bv, L0_conv_se_w1, L0_conv_se_w2,
           L0_conv_gamma, L1_ffn_router_w, L1_ffn_router_b, L1_ffn_expert_w, L1_ffn_expert_b):
    import numpy as np
    import concourse.bacc as bacc
    from concourse.bass_utils import run_bass_kernel_spmd

    laid = {
        "x": np.asarray(x).reshape(B, C, NTOK),
        "wq": np.asarray(L0_conv_Wq).T, "wk": np.asarray(L0_conv_Wk).T, "wv": np.asarray(L0_conv_Wv).T,
        "bq": np.asarray(L0_conv_bq).reshape(C, 1), "bk": np.asarray(L0_conv_bk).reshape(C, 1),
        "bv": np.asarray(L0_conv_bv).reshape(C, 1),
        "w1": np.asarray(L0_conv_se_w1).T, "w2": np.asarray(L0_conv_se_w2).T,
        "gamma": np.broadcast_to(np.asarray(L0_conv_gamma).reshape(1, 1), (C, 1)),
        "rw": np.asarray(L1_ffn_router_w),
        "rb": np.broadcast_to(np.asarray(L1_ffn_router_b).reshape(1, E), (C, E)),
        "ew": np.asarray(L1_ffn_expert_w).transpose(1, 0, 2).reshape(C, E * C),
        "eb": np.asarray(L1_ffn_expert_b).reshape(1, E * C),
    }
    nc = bacc.Bacc("TRN2", target_bir_lowering=False, num_devices=1)
    arrays, args = {}, []
    for name in _INS:
        arrays[name] = np.ascontiguousarray(laid[name])
        args.append(nc.dram_tensor(name, arrays[name].shape, F32, kind="ExternalInput").ap())
    out = nc.dram_tensor("y", (B, C, NTOK), F32, kind="ExternalOutput").ap()
    build(nc, *args, out)
    r = run_bass_kernel_spmd(nc, [arrays], core_ids=[0])
    return r.results[0]["y"].reshape(B, C, 48, 48)
```

```python
import concourse.bass as bass
from concourse import mybir
from contextlib import ExitStack

F32 = mybir.dt.float32
F32R = mybir.dt.float32r
ALU = mybir.AluOpType
ACT = mybir.ActivationFunctionType
AX = mybir.AxisListType

B, C, NTOK = 8, 128, 48 * 48
E, RED = 8, 8
TILE = 128
NT = NTOK // TILE
BW = 3 * TILE
NB = NTOK // BW
TPB = BW // TILE
LW = 2 * BW
LB = NTOK // LW
CHUNK = 512
QC = [(a, min(CHUNK, NTOK - a)) for a in range(0, NTOK, CHUNK)]
GN_EPS, LN_EPS = 1e-5, 1e-5
SHIFT = C / 2.0
LAG = 2
LAG0 = 3
PTS = 6
RING0 = 6
ROW_BUFFER = {(0, 0): 0, (0, 1): 1, (1, 0): 2, (1, 1): 3, (2, 0): 4, (2, 1): 4}


def last_tile(c):
    a, w = QC[c]
    return (a + w) // TILE - 1


def chunk_of(j):
    return j * TILE // CHUNK


VT_SLOTS = [2, 5, 8, 11, 16, 17]


def attention0(n, j):
    s = []
    k = j % 6
    row = n * TPB + j // 6
    last = len(QC) - 1
    if n < NB and k == last:
        s += [("scores", n, row % TPB, last), ("row_max", n, row % TPB)]
    if n >= 1:
        s.append(("pt", n - 1, j))
    if n >= 1 and j == 9:
        s.append(("baset", n - 1))
    if n + 1 < NB and j == 13:
        s.append(("qproj", n + 1))
    if n >= 2:
        s += {4: [("ot", n - 2)], 15: [("tnt", n - 2)]}.get(j, [])
    if n >= 1:
        g = (n - 1) * NT + j - LAG0
        if g >= 0:
            s.append(("pv", g // NT, g % NT))
        if g >= 0 and g % NT == NT - 1:
            s.append(("oevac", g // NT))
    if n < NB and k < last:
        s.append(("scores", n, row % TPB, k))
    if n < NB and k >= last:
        s.append(("exp", n, row % TPB, k - last))
    if k < 3 and 1 <= row <= NB * TPB:
        s.append(("exp", (row - 1) // TPB, (row - 1) % TPB, k + 2))
    if n >= 2:
        s += {2: [("rowsum", n - 2)], 5: [("ln", n - 2)], 10: [("lnapply", n - 2)], 15: [("lnhigh", n - 2)],
              16: [("lnlow", n - 2)]}.get(j, [])
    if n == 0 and j % 3 == 0 and j:
        s.append(("vproj", j // 3))
    if n == 0 and j in VT_SLOTS:
        s.append(("vt", VT_SLOTS.index(j)))
    return s


STATISTICS = [("stat", m) for m in range(NB)] + [("gn_mean",), ("gn_dev",), ("gn_var",), ("gn_norm",), ("se_in",),
                                                 ("se_out",)]
NORMALISE = [("xgnorm", u) for u in range(LB)]
PROJECTIONS = [[("xg", 0)], [("xg", 1), ("kproj", 0), ("kproj", 1)],
               [("xg", 2), ("kproj", 2), ("kproj", 3), ("qproj", 0), ("vproj", 0)],
               [("kproj", 4), ("kproj", 5)]]
STAGE0 = PROJECTIONS + [attention0(0, j) for j in range(NT)]
for u in range(LB):
    STAGE0[5 + 6 * u].append(("base", u))
HEAD = STATISTICS + NORMALISE + [step for steps in STAGE0 for step in steps]


def moe(m, at, stride):
    s = {0: [("o1t", m)], 1: [("uln", m)], 2: [("uapply", m)], 3: [("ut", m)], 4: [("router", m)],
         7 + 2 * stride: [("yt", m)]}
    for k in range(TPB):
        s[6 + k * stride] = [("expert", m, k, 0), ("expert", m, k, 1)]
    return {at + i: steps for i, steps in s.items()}


def plan():
    s = [step for n in range(1, NB + 1) for j in range(NT) for step in attention0(n, j)]
    m = NB - 1
    beside = {0: [("pv", m, NT - 3), ("pv", m, NT - 2)], 1: [("pv", m, NT - 1), ("oevac", m), ("rowsum", m)],
              2: [("ot", m)], 3: [("ln", m)], 4: [("lnapply", m)], 6: [("lnhigh", m)], 7: [("lnlow", m)], 8: [("tnt", m)]}
    for slot, step in zip([9, 10, 11, 12, 13, 14, 15, 17, 19, 20, 23, 25, 27, 36, 45], STATISTICS + NORMALISE):
        beside.setdefault(slot, []).append(step)
    for block, (at, stride) in enumerate([(20, 2), (29, 2), (38, 2), (47, 1), (56, 1), (62, 1)]):
        for slot, steps in moe(block, at, stride).items():
            beside.setdefault(slot, []).extend(steps)
    for slot, steps in enumerate(STAGE0):
        beside.setdefault(LB * NT + slot, []).extend(steps)
    for w in range(max(beside) + 1):
        if w < LB * NT:
            s.append(("s1", w))
        if LAG <= w < LB * NT + LAG:
            s.append(("pv1", w - LAG))
            if (w - LAG) % NT == NT - 1:
                s.append(("o1evac", (w - LAG) // NT))
        s += beside.get(w, [])
    return s


PLAN = plan()
POSITION = {step: i for i, step in enumerate(PLAN)}
RAISES = {
    "stat": [], "gn_mean": ["gn_stats_ready"], "gn_dev": ["ring_full", "gn_dev_ready"],
    "gn_var": ["ring_full", "gn_var_ready", "gn_rstd_ready"], "gn_norm": ["se_in_ready"],
    "se_in": ["ring_full", "se_hidden_ready"], "se_out": ["ring_full", "se_exp_ready"],
    "xgnorm": ["xg_norm_ready"], "xg": ["xg_hi_ready", "xg_lo_ready"], "base": ["base_done"],
    "kproj": ["kproj_done", "k_hi_ready", "k_lo_ready"], "vproj": ["vproj_done", "v_chan_ready"],
    "vt": ["ring_full", "v_hi_ready", "v_lo_ready"], "baset": ["ring_full", "base_tok_ready"],
    "qproj": ["ring_full", "q_hi_ready", "q_lo_ready"],
    "scores": ["scores_done"], "row_max": ["row_max_ready"], "exp": ["p_rows_ready"],
    "pt": ["ring_full", "pt_hi_ready", "pt_lo_ready"], "pv": ["pv_done"], "oevac": ["o_chan_ready"],
    "rowsum": [], "ot": ["ring_full", "o_added"], "ln": ["ln_var_ready", "ln_rstd_ready"],
    "lnapply": ["tn_tok_ready"], "lnhigh": ["tn_hi_ready"], "lnlow": ["tn_lo_ready"],
    "tnt": ["ring_full", "tnt_hi_ready", "tnt_lo_ready"],
    "s1": ["s1_done", "p1_exp_ready", "p1_hi_ready", "p1_lo_ready"], "pv1": ["pv1_done"], "o1evac": ["o1_chan_ready"],
    "o1t": ["ring_full", "o1_added"], "uln": ["u_var_ready", "u_rstd_ready"], "uapply": ["u_tok_ready"],
    "ut": ["ring_full", "u_hi_ready", "u_lo_ready"],
    "router": ["ring_full", "logit_max_ready", "gate_exp_ready", "gates_ready"],
    "expert": ["ring_full", "expert_added"], "yt": ["ring_full", "y_chan_ready"],
}
LAST = {"gn_dev": "gn_dev_ready", "gn_var": "gn_var_ready", "se_in": "se_hidden_ready", "se_out": "se_exp_ready",
        "vt": "v_lo_ready", "baset": "base_tok_ready",
        "qproj": "q_lo_ready", "pt": "pt_lo_ready", "ot": "o_added", "tnt": "tnt_lo_ready", "o1t": "o1_added",
        "ut": "u_lo_ready", "router": "logit_max_ready", "expert": "expert_added", "yt": "y_chan_ready"}
CHAINED = {"stat": 1, "gn_dev": 2, "se_out": 5, "rowsum": 3, "ot": 2, "ln": 6, "o1t": 5, "uln": 6, "router": 11,
           "expert": 4, "scores": 1, "lnapply": 2, "uapply": 2}


def linked(step):
    return CHAINED.get(step[0], 0) - (step[0] == "expert" and step[3] == 0)


def count(steps):
    order, links, total = {name: {} for names in RAISES.values() for name in names}, {}, 0
    for step in steps:
        for name in RAISES[step[0]]:
            order[name][step] = len(order[name]) + 1
        links[step] = total
        total += linked(step)
    return order, links, total


HEAD_ORDER, HEAD_LINKS, HEAD_CHAIN = count(HEAD)
ORDER, LINKS, CHAIN = count(PLAN)
IN_HEAD = {name: len(steps) for name, steps in HEAD_ORDER.items()}
PER = {name: len(steps) for name, steps in ORDER.items()}
HEAD_RING = list(HEAD_ORDER["ring_full"])
RING = list(ORDER["ring_full"])
assert len(HEAD_RING) % 2 == 0 and len(RING) % 2 == 0 and HEAD_RING[-2:] == RING[-2:]
STARTED = {"pv1_done", "o1_chan_ready", "expert_added"}


def build(nc, x, wq, wk, wv, bq, bk, bv, w1, w2, gamma, rw, rb, ew, eb, y):
    ctx = ExitStack()
    with ctx:
        def sb(name, shape, dt=F32):
            return ctx.enter_context(nc.sbuf_tensor(name, shape, dt))

        ps = ctx.enter_context(nc.psum_tensor("ps", [128, 8, 512], F32))

        ident = sb("ident", [128, 128])
        group = sb("group", [128, 128])
        ones = sb("ones", [128, 128], F32R)
        lower = sb("lower", [128, E, E])
        minus_half = sb("minus_half", [128, TPB])
        shift = sb("shift", [128, 1])
        plus_one = sb("plus_one", [128, 1])
        minus_one = sb("minus_one", [128, 1])
        w_hi = sb("w_hi", [128, 3, 128], F32R)
        w_lo = sb("w_lo", [128, 3, 128], F32R)
        biases = sb("biases", [128, 4])
        w1_sb = sb("w1_sb", [128, RED])
        w2_sb = sb("w2_sb", [RED, 128])
        rw_hi = sb("rw_hi", [128, E], F32R)
        rw_lo = sb("rw_lo", [128, E], F32R)
        rb_sb = sb("rb_sb", [128, E])
        ew_hi = sb("ew_hi", [128, E * 128], F32R)
        ew_lo = sb("ew_lo", [128, E * 128], F32R)
        eb_rows = sb("eb_rows", [128, E * 128], F32R)

        x_chan = sb("x_chan", [128, NTOK])
        t_tok = sb("t_tok", [128, NT, 128])
        xt_hi = sb("xt_hi", [128, NTOK], F32R)
        xt_lo = sb("xt_lo", [128, NTOK], F32R)
        k_hi = sb("k_hi", [128, NTOK], F32R)
        k_lo = sb("k_lo", [128, NTOK], F32R)
        v_hi = sb("v_hi", [128, NT, 128], F32R)
        v_lo = sb("v_lo", [128, NT, 128], F32R)
        q_hi = sb("q_hi", [128, 2, BW], F32R)
        q_lo = sb("q_lo", [128, 2, BW], F32R)
        p_rows = sb("p_rows", [128, 5, NTOK])
        pt_hi = sb("pt_hi", [128, PTS, BW], F32R)
        pt_lo = sb("pt_lo", [128, PTS, BW], F32R)
        o_chan = sb("o_chan", [128, BW])
        tn_tok = sb("tn_tok", [128, TPB, 128])
        tn_hi = sb("tn_hi", [128, NT, 128], F32R)
        tn_lo = sb("tn_lo", [128, NT, 128], F32R)
        u_tok = sb("u_tok", [128, TPB, 128])
        u_hi = sb("u_hi", [128, BW], F32R)
        u_lo = sb("u_lo", [128, BW], F32R)
        acc = sb("acc", [128, 2, TPB, 128])
        acc_odd = sb("acc_odd", [128, 128])
        y_out = sb("y_out", [128, 2, BW])
        p1_f = p_rows[:, 0, 0:2 * LW].rearrange("p (s w) -> p s w", s=2)
        o1_chan = p_rows[:, 3, 0:2 * LW].rearrange("p (s w) -> p s w", s=2)
        xg_f = p_rows[:, 4, :].rearrange("p (s w) -> p s w", s=LB)
        v_chan = p_rows[:, 1, 0:2 * BW].rearrange("p (s w) -> p s w", s=2)
        p1_hi = pt_hi[:, :, :].rearrange("p (s a) w -> p s (a w)", a=2)
        p1_lo = pt_lo[:, :, :].rearrange("p (s a) w -> p s (a w)", a=2)
        w_stage = p_rows[:, 0, 0:384].rearrange("p (a w) -> p a w", a=3)
        rw_stage = p_rows[:, 0, 384:384 + E]
        ew_stage = p_rows[:, 1, 0:E * 128]
        eb_stage = p_rows[:, 2, 0:E * 128]
        ones_stage = p_rows[:, 3, 0:128]

        wait_carrier = sb("wait_carrier", [128, 1])
        gn_raw = sb("gn_raw", [128, NB, 6])
        gn_mv = sb("gn_mv", [128, 2])
        gs = sb("gs", [128, 12])
        gmean, gdev, gsq, gve, grstd, se_in = [gs[:, i:i + 1] for i in range(6)]
        se_h, se_e, ysig, yscale, yshift, se_tmp = [gs[:, i:i + 1] for i in range(6, 12)]
        mx = sb("mx", [128, len(QC)])
        negmax = sb("negmax", [128, 2])
        dparts = sb("dparts", [128, NB, TPB, len(QC)])
        rg = sb("rg", [128, 3, TPB])
        ln_raw = sb("ln_raw", [128, TPB, 6])
        ln_mv = sb("ln_mv", [128, TPB, 2])
        ln_ve = sb("ln_ve", [128, TPB])
        ln_rs = sb("ln_rs", [128, TPB])
        r1 = sb("r1", [128, 3, TPB])
        u_raw = sb("u_raw", [128, TPB, 6])
        u_mv = sb("u_mv", [128, TPB, 2])
        u_ve = sb("u_ve", [128, TPB])
        u_rs = sb("u_rs", [128, TPB])
        logits = sb("logits", [128, TPB, E])
        centred = sb("centred", [128, TPB, E])
        gexp = sb("gexp", [128, TPB, E])
        lmax = sb("lmax", [128, TPB])
        cmp_gt = sb("cmp_gt", [128, TPB, E, E])
        cmp_ge = sb("cmp_ge", [128, TPB, E, E])
        rank = sb("rank", [128, TPB, E])
        gsum = sb("gsum", [128, 2, TPB])
        gates = sb("gates", [128, 2, TPB, E])

        def signal(name):
            return ctx.enter_context(nc.semaphore(name))

        gn_stats_ready = signal("gn_stats_ready")
        ring_full = signal("ring_full")
        kproj_done = signal("kproj_done")
        vproj_done = signal("vproj_done")
        gn_dev_ready = signal("gn_dev_ready")
        gn_var_ready = signal("gn_var_ready")
        gn_rstd_ready = signal("gn_rstd_ready")
        se_in_ready = signal("se_in_ready")
        se_hidden_ready = signal("se_hidden_ready")
        se_exp_ready = signal("se_exp_ready")
        xg_norm_ready = signal("xg_norm_ready")
        xg_hi_ready = signal("xg_hi_ready")
        xg_lo_ready = signal("xg_lo_ready")
        base_done = signal("base_done")
        k_hi_ready = signal("k_hi_ready")
        k_lo_ready = signal("k_lo_ready")
        v_chan_ready = signal("v_chan_ready")
        base_tok_ready = signal("base_tok_ready")
        v_hi_ready = signal("v_hi_ready")
        v_lo_ready = signal("v_lo_ready")
        q_hi_ready = signal("q_hi_ready")
        q_lo_ready = signal("q_lo_ready")
        scores_done = signal("scores_done")
        row_max_ready = signal("row_max_ready")
        p_rows_ready = signal("p_rows_ready")
        pt_hi_ready = signal("pt_hi_ready")
        pt_lo_ready = signal("pt_lo_ready")
        pv_done = signal("pv_done")
        o_chan_ready = signal("o_chan_ready")
        o_added = signal("o_added")
        ln_var_ready = signal("ln_var_ready")
        ln_rstd_ready = signal("ln_rstd_ready")
        tn_tok_ready = signal("tn_tok_ready")
        tn_hi_ready = signal("tn_hi_ready")
        tn_lo_ready = signal("tn_lo_ready")
        tnt_hi_ready = signal("tnt_hi_ready")
        tnt_lo_ready = signal("tnt_lo_ready")
        s1_done = signal("s1_done")
        p1_exp_ready = signal("p1_exp_ready")
        p1_hi_ready = signal("p1_hi_ready")
        p1_lo_ready = signal("p1_lo_ready")
        pv1_done = signal("pv1_done")
        o1_chan_ready = signal("o1_chan_ready")
        o1_added = signal("o1_added")
        u_var_ready = signal("u_var_ready")
        u_rstd_ready = signal("u_rstd_ready")
        u_tok_ready = signal("u_tok_ready")
        u_hi_ready = signal("u_hi_ready")
        u_lo_ready = signal("u_lo_ready")
        logit_max_ready = signal("logit_max_ready")
        gate_exp_ready = signal("gate_exp_ready")
        gates_ready = signal("gates_ready")
        expert_added = signal("expert_added")
        y_chan_ready = signal("y_chan_ready")
        x_loaded = signal("x_loaded")
        w_loaded = signal("w_loaded")
        consts_made = signal("consts_made")
        eb_zeroed = signal("eb_zeroed")
        w_split = signal("w_split")
        vector_chain = signal("vector_chain")
        y_stored = [signal(f"y_stored{i}") for i in range(2)]
        signals = {s.name: s for s in (base_tok_ready, expert_added, gn_dev_ready, gn_var_ready,
                                       logit_max_ready, o_added, o1_added, pt_lo_ready, q_lo_ready,
                                       se_exp_ready, se_hidden_ready, tnt_lo_ready, u_lo_ready,
                                       v_lo_ready, y_chan_ready)}
        block = ctx.enter_context(nc.Block())

        N_WLOADS = 12
        W_SPLITS = 9

        wait_value = {}

        def value(eng, b, per_batch, count):
            if isinstance(b, int):
                return b * per_batch + count
            if eng.engine not in wait_value:
                wait_value[eng.engine] = eng.alloc_register("wait_value")
            eng.reg_mul(wait_value[eng.engine], b, per_batch)
            eng.reg_add(wait_value[eng.engine], wait_value[eng.engine], count)
            return wait_value[eng.engine]

        here = {}

        def at(eng, b, sem, *step):
            start = sem.name in STARTED
            if b is None:
                return HEAD_ORDER[sem.name][step] + start
            count = start + IN_HEAD[sem.name] + ORDER[sem.name][step]
            if POSITION[step] > here.get(eng.engine, len(PLAN)):
                count -= PER[sem.name]
                assert count == HEAD_ORDER[sem.name][step] + start
            return value(eng, b, PER[sem.name], count)

        def before(eng, b, sem):
            return value(eng, b, PER[sem.name], (sem.name in STARTED) + IN_HEAD[sem.name])

        def ring_index(b, step):
            return (HEAD_ORDER if b is None else ORDER)["ring_full"][step] - 1

        def key_bank(m):
            return ps[:, m % 5, 0:BW]

        def ring_bank(b, step):
            return ps[:, RING0 + ring_index(b, step) % 2, :]

        def filled(eng, b, step):
            return at(eng, b, ring_full, *step)

        def reader(b, step):
            return signals[LAST[(HEAD_RING if b is None else RING)[ring_index(b, step) - 2][0]]]

        def freed(eng, b, step):
            i = ring_index(b, step)
            if i >= 2:
                return at(eng, b, reader(b, step), *(HEAD_RING if b is None else RING)[i - 2])
            return before(eng, b, reader(b, step))

        def chained(b, step, links):
            if b is None:
                return HEAD_LINKS[step] + links
            return value(nc.vector, b, CHAIN, HEAD_CHAIN + LINKS[step] + links)

        def tiled(ap):
            return ap.rearrange("p (t w) -> p t w", w=128)

        @block.sync
        def _(sp):
            for stored in y_stored:
                sp.sem_inc(stored, 1)
            sp.dma_start(x_chan[:, :], x[0]).then_inc(x_loaded, 16)
            sp.dma_start(w_stage[:, 0, :], wq).then_inc(w_loaded, 16)
            sp.dma_start(w_stage[:, 1, :], wk).then_inc(w_loaded, 16)
            sp.dma_start(w_stage[:, 2, :], wv).then_inc(w_loaded, 16)
            sp.dma_start(biases[:, 0:1], bq).then_inc(w_loaded, 16)
            sp.dma_start(biases[:, 1:2], bk).then_inc(w_loaded, 16)
            sp.dma_start(biases[:, 2:3], bv).then_inc(w_loaded, 16)
            sp.dma_start(biases[:, 3:4], gamma).then_inc(w_loaded, 16)
            sp.dma_start(w1_sb[:, :], w1).then_inc(w_loaded, 16)
            sp.dma_start(w2_sb[:, :], w2).then_inc(w_loaded, 16)
            sp.dma_start(rw_stage, rw).then_inc(w_loaded, 16)
            sp.dma_start(rb_sb[:, :], rb).then_inc(w_loaded, 16)
            sp.dma_start(ew_stage, ew).then_inc(w_loaded, 16)
            sp.wait_ge(eb_zeroed, 1)
            sp.dma_start(eb_stage[0:1, :], eb).then_inc(w_loaded, 16)
            sp.dma_start(eb_stage[32:33, :], eb).then_inc(w_loaded, 16)

            def store(b):
                for mb in range(NB):
                    sp.wait_ge(y_chan_ready, at(sp, b, y_chan_ready, "yt", mb))
                    sp.dma_start(y[bass.ds(b, 1), :, mb * BW:(mb + 1) * BW].rearrange("a c n -> (a c) n"),
                                 y_out[:, mb % 2, :]).then_inc(y_stored[mb % 2], 16)

            with sp.Fori(0, B - 1) as b:
                sp.wait_ge(ring_full, filled(sp, b, ("baset", NB - 1)))
                sp.dma_start(x_chan[:, :], x[bass.ds(b + 1, 1)].rearrange("a c n -> (a c) n")).then_inc(x_loaded, 16)
                store(b)
            sp.wait_ge(ring_full, filled(sp, B - 1, ("baset", NB - 1)))
            sp.dma_start(x_chan[:, :], x[B - 1]).then_inc(x_loaded, 16)
            store(B - 1)
            for stored in y_stored:
                sp.wait_ge(stored, 16 * B * (NB // 2) + 1)

        @block.gpsimd
        def _(pool):
            pool.memset(ident[:, :], 0.0).then_inc(consts_made, 1)
            pool.memset(group[:, :], 1.0 / 4).then_inc(consts_made, 1)
            pool.memset(lower[:, :, :], 1.0).then_inc(consts_made, 1)
            pool.memset(minus_half[:, :], -0.5).then_inc(consts_made, 1)
            pool.memset(shift[:, :], -SHIFT).then_inc(consts_made, 1)
            pool.memset(plus_one[:, :], 1.0).then_inc(consts_made, 1)
            pool.memset(minus_one[:, :], -1.0).then_inc(consts_made, 1)
            pool.wait_ge(consts_made, 7)
            pool.affine_select(out=ident[:, :], in_=ident[:, :], compare_op=ALU.not_equal, fill=1.0, base=0,
                               pattern=[[-1, 128]], channel_multiplier=1).then_inc(consts_made, 1)
            pool.affine_select(out=group[:, :], in_=group[:, :], compare_op=ALU.is_ge, fill=0.0, base=0,
                               pattern=[[-4, 32], [0, 4]], channel_multiplier=1).then_inc(consts_made, 1)
            pool.affine_select(out=lower[:, :, :], in_=lower[:, :, :], compare_op=ALU.is_gt, fill=0.0, base=0,
                               pattern=[[1, E], [-1, E]], channel_multiplier=0).then_inc(consts_made, 1)
            pool.wait_ge(consts_made, 10)
            pool.affine_select(out=group[:, :], in_=group[:, :], compare_op=ALU.is_ge, fill=0.0, base=3,
                               pattern=[[4, 32], [0, 4]], channel_multiplier=-1).then_inc(consts_made, 1)
            pool.wait_ge(consts_made, 11)

            def take(step, b):
                kind = step[0]
                if kind == "gn_var":
                    pool.wait_ge(gn_var_ready, at(pool, b, gn_var_ready, *step))
                    pool.tensor_tensor(grstd, gve, minus_half[:, 0:1], ALU.pow).then_inc(gn_rstd_ready, 1)
                if kind == "ln":
                    pool.wait_ge(ln_var_ready, at(pool, b, ln_var_ready, *step))
                    pool.tensor_tensor(ln_rs[:, :], ln_ve[:, :], minus_half[:, :], ALU.pow).then_inc(ln_rstd_ready, 1)
                if kind == "uln":
                    pool.wait_ge(u_var_ready, at(pool, b, u_var_ready, *step))
                    pool.tensor_tensor(u_rs[:, :], u_ve[:, :], minus_half[:, :], ALU.pow).then_inc(u_rstd_ready, 1)

            for step in HEAD:
                take(step, None)
            with pool.Fori(0, B) as b:
                for i, step in enumerate(PLAN):
                    here[pool.engine] = i
                    take(step, b)

        @block.scalar
        def _(act):
            act.sem_inc(o1_chan_ready, 1)
            act.wait_ge(w_split, W_SPLITS)
            act.wait_ge(consts_made, 11)

            def take(step, b):
                kind = step[0]
                if kind == "se_out":
                    act.wait_ge(ring_full, filled(act, b, step))
                    act.activation(se_e, ring_bank(b, step)[:, 0:1], ACT.Exp, scale=-1.0).then_inc(se_exp_ready, 1)
                elif kind == "xg":
                    u = step[1]
                    act.wait_ge(xg_norm_ready, at(act, b, xg_norm_ready, "xgnorm", u))
                    if u == 0 and b is not None:
                        act.wait_ge(s1_done, at(act, b, s1_done, "s1", LB * NT - 1))
                    act.activation(xt_hi[:, u * LW:(u + 1) * LW], xg_f[:, u, :], ACT.Copy)\
                        .then_inc(xg_hi_ready, 1)
                elif kind == "base":
                    u = step[1]
                    act.wait_ge(xg_norm_ready, at(act, b, xg_norm_ready, "xgnorm", LB - 1))
                    cols = slice(u * LW, (u + 1) * LW)
                    act.activation(x_chan[:, cols], x_chan[:, cols], ACT.Identity, bias=yshift, scale=yscale)\
                        .then_inc(base_done, 1)
                elif kind == "kproj":
                    m = step[1]
                    act.wait_ge(kproj_done, at(act, b, kproj_done, *step))
                    act.activation(k_hi[:, m * BW:(m + 1) * BW], key_bank(m), ACT.Identity,
                                   bias=biases[:, 1:2]).then_inc(k_hi_ready, 1)
                elif kind == "vproj":
                    m = step[1]
                    act.wait_ge(vproj_done, at(act, b, vproj_done, *step))
                    if m >= 2:
                        act.wait_ge(ring_full, filled(act, b, ("vt", m - 2)))
                    act.activation(v_chan[:, m % 2, :], ps[:, 5, 0:BW], ACT.Identity,
                                   bias=biases[:, 2:3]).then_inc(v_chan_ready, 1)
                elif kind == "vt":
                    m = step[1]
                    act.wait_ge(ring_full, filled(act, b, step))
                    act.activation(v_hi[:, TPB * m:TPB * (m + 1), :], tiled(ring_bank(b, step)[:, 0:BW]), ACT.Copy)\
                        .then_inc(v_hi_ready, 1)
                elif kind == "baset":
                    m = step[1]
                    act.wait_ge(ring_full, filled(act, b, step))
                    if m == 0:
                        act.wait_ge(expert_added, before(act, b, expert_added))
                    act.activation(t_tok[:, TPB * m:TPB * (m + 1), :], tiled(ring_bank(b, step)[:, 0:BW]), ACT.Copy)\
                        .then_inc(base_tok_ready, 1)
                elif kind == "qproj":
                    n = step[1]
                    act.wait_ge(ring_full, filled(act, b, step))
                    act.activation(q_hi[:, n % 2, :], ring_bank(b, step)[:, 0:BW], ACT.Identity,
                                   bias=biases[:, 0:1]).then_inc(q_hi_ready, 1)
                elif kind == "exp":
                    n, r, c = step[1:]
                    a, w = QC[c]
                    if c == 0:
                        act.wait_ge(row_max_ready, at(act, b, row_max_ready, "row_max", n, r))
                        if n >= 2 and r == 0:
                            act.wait_ge(ring_full, filled(act, b, ("pt", n - 2, NT - 1)))
                        if n == 0 and r == 0 and b is not None:
                            act.wait_ge(p1_hi_ready, at(act, b, p1_hi_ready, "s1", LB * NT - 1))
                            act.wait_ge(p1_lo_ready, at(act, b, p1_lo_ready, "s1", LB * NT - 1))
                            act.wait_ge(o_added, at(act, b, o_added, "ot", NB - 1))
                        if n == 1 and r == 0:
                            act.wait_ge(ring_full, before(act, b, ring_full))
                        if n == 0 and r == 2:
                            act.wait_ge(xg_lo_ready, at(act, b, xg_lo_ready, "xg", LB - 1))
                    if r == 2 and n >= 1:
                        act.wait_ge(ring_full, filled(act, b, ("pt", n - 1, last_tile(c))))
                    act.activation(p_rows[:, ROW_BUFFER[r, n % 2], a:a + w], ps[:, c, 0:w], ACT.Exp,
                                   bias=negmax[:, r % 2:r % 2 + 1],
                                   accum_out=dparts[:, n, r, c:c + 1]).then_inc(p_rows_ready, 1)
                elif kind == "pt":
                    n, j = step[1:]
                    g = n * NT + j
                    slot = g % PTS
                    act.wait_ge(ring_full, filled(act, b, step))
                    if g >= PTS:
                        act.wait_ge(pv_done, at(act, b, pv_done, "pv", (g - PTS) // NT, (g - PTS) % NT))
                    else:
                        act.wait_ge(pv1_done, before(act, b, pv1_done))
                    act.activation(pt_hi[:, slot, :], ring_bank(b, step)[:, 0:BW], ACT.Copy)\
                        .then_inc(pt_hi_ready, 1)
                elif kind == "oevac":
                    m = step[1]
                    act.wait_ge(pv_done, at(act, b, pv_done, "pv", m, NT - 1))
                    if m >= 1:
                        act.wait_ge(ring_full, filled(act, b, ("ot", m - 1)))
                    act.activation(o_chan[:, :], ps[:, 5, 0:BW], ACT.Copy).then_inc(o_chan_ready, 1)
                elif kind == "lnhigh":
                    m = step[1]
                    act.wait_ge(tn_tok_ready, at(act, b, tn_tok_ready, "lnapply", m))
                    if m == 0:
                        act.wait_ge(pv1_done, before(act, b, pv1_done))
                    act.activation(tn_hi[:, TPB * m:TPB * (m + 1), :], tn_tok[:, :, :], ACT.Identity,
                                   bias=plus_one[:, :])\
                        .then_inc(tn_hi_ready, 1)
                elif kind == "tnt":
                    m = step[1]
                    act.wait_ge(ring_full, filled(act, b, step))
                    act.activation(xt_hi[:, m * BW:(m + 1) * BW], ring_bank(b, step)[:, 0:BW], ACT.Copy)\
                        .then_inc(tnt_hi_ready, 1)
                elif kind == "s1":
                    w = step[1]
                    ib, j = divmod(w, NT)
                    act.wait_ge(s1_done, at(act, b, s1_done, *step))
                    if w == 0:
                        act.wait_ge(ring_full, filled(act, b, ("pt", NB - 1, NT - 1)))
                    if w >= 2:
                        act.wait_ge(p1_lo_ready, at(act, b, p1_lo_ready, "s1", w - 2))
                    act.activation(p1_f[:, w % 2, :].rearrange("p (s w) -> p s w", s=2),
                                   ps[:, 2 * (w % 2):2 * (w % 2) + 2, 0:BW], ACT.Exp, bias=shift[:, :])\
                        .then_inc(p1_exp_ready, 1)
                    if w >= 3:
                        act.wait_ge(pv1_done, at(act, b, pv1_done, "pv1", w - 3))
                    else:
                        act.wait_ge(pv_done, at(act, b, pv_done, "pv", NB - 1, NT - PTS + 2 * w + 1))
                    act.wait_ge(p1_exp_ready, at(act, b, p1_exp_ready, *step))
                    act.activation(p1_hi[:, w % 3, :], p1_f[:, w % 2, :], ACT.Copy).then_inc(p1_hi_ready, 1)
                elif kind == "o1evac":
                    ib = step[1]
                    act.wait_ge(pv1_done, at(act, b, pv1_done, "pv1", ib * NT + NT - 1))
                    if ib >= 2:
                        act.wait_ge(ring_full, filled(act, b, ("o1t", 2 * (ib - 2) + 1)))
                    act.activation(o1_chan[:, ib % 2, :].rearrange("p (s w) -> p s w", s=2), ps[:, 4:6, 0:BW],
                                   ACT.Copy).then_inc(o1_chan_ready, 1)
                elif kind == "ut":
                    act.wait_ge(ring_full, filled(act, b, step))
                    act.activation(u_hi[:, :], ring_bank(b, step)[:, 0:BW], ACT.Copy).then_inc(u_hi_ready, 1)
                elif kind == "router":
                    act.wait_ge(logit_max_ready, at(act, b, logit_max_ready, *step))
                    act.activation(gexp[:, :, :], centred[:, :, :], ACT.Exp).then_inc(gate_exp_ready, 1)
                elif kind == "yt":
                    mb = step[1]
                    act.wait_ge(ring_full, filled(act, b, step))
                    act.wait_ge(y_stored[mb % 2], value(act, b, 16 * (NB // 2), 16 * (mb // 2) + 1))
                    act.activation(y_out[:, mb % 2, :], ring_bank(b, step)[:, 0:BW], ACT.Identity,
                                   bias=minus_one[:, :])\
                        .then_inc(y_chan_ready, 1)

            for step in HEAD:
                take(step, None)
            with act.Fori(0, B) as b:
                for i, step in enumerate(PLAN):
                    here[act.engine] = i
                    take(step, b)

        @block.vector
        def _(dve):
            dve.sem_inc(expert_added, 1)
            dve.memset(eb_stage, 0.0).then_inc(eb_zeroed, 1)
            dve.wait_ge(w_loaded, 16 * (N_WLOADS + 2))
            dve.tensor_copy(w_hi[:, :, :], w_stage).then_inc(w_split, 1)
            dve.tensor_copy(rw_hi[:, :], rw_stage).then_inc(w_split, 1)
            dve.tensor_copy(ew_hi[:, :], ew_stage).then_inc(w_split, 1)
            dve.tensor_copy(eb_rows[:, :], eb_stage).then_inc(w_split, 1)
            dve.wait_ge(w_split, 4)
            dve.tensor_tensor(w_lo[:, :, :], w_stage, w_hi[:, :, :], ALU.subtract).then_inc(w_split, 1)
            dve.tensor_tensor(rw_lo[:, :], rw_stage, rw_hi[:, :], ALU.subtract).then_inc(w_split, 1)
            dve.tensor_tensor(ew_lo[:, :], ew_stage, ew_hi[:, :], ALU.subtract).then_inc(w_split, 1)
            dve.tensor_tensor(eb_rows[32:64, :], eb_stage[32:64, :], eb_rows[32:64, :], ALU.subtract)\
                .then_inc(w_split, 1)
            dve.memset(ones_stage, 1.0).then_inc(eb_zeroed, 1)
            dve.wait_ge(eb_zeroed, 2)
            dve.tensor_copy(ones[:, :], ones_stage).then_inc(w_split, 1)
            dve.wait_ge(w_split, W_SPLITS)
            dve.wait_ge(consts_made, 11)

            def take(step, b):
                kind = step[0]
                links = [0]

                def link(ins):
                    links[0] += 1
                    ins.then_inc(vector_chain, 1)

                if kind == "stat":
                    m = step[1]
                    if m == 0:
                        dve.wait_ge(x_loaded, 16 if b is None else value(dve, b, 16, 32))
                    link(dve.bn_stats(gn_raw[:, m, :], x_chan[:, m * BW:(m + 1) * BW]))
                elif kind == "gn_mean":
                    dve.wait_ge(vector_chain, chained(b, step, 0))
                    dve.memset(wait_carrier[:, :], 0.0)
                    dve.bn_aggr(gn_mv[:, :], gn_raw[:, :, :]).then_inc(gn_stats_ready, 1)
                elif kind == "gn_dev":
                    dve.wait_ge(gn_stats_ready, at(dve, b, gn_stats_ready, "gn_mean"))
                    dve.wait_ge(ring_full, filled(dve, b, step))
                    bank = ring_bank(b, step)[:, 0:1]
                    link(dve.tensor_copy(gmean, bank))
                    link(dve.tensor_tensor(gdev, gn_mv[:, 0:1], bank, ALU.subtract))
                    dve.wait_ge(vector_chain, chained(b, step, links[0]))
                    dve.scalar_tensor_tensor(out=gsq, in0=gdev, scalar=gdev, in1=gn_mv[:, 1:2], op0=ALU.mult,
                                             op1=ALU.add).then_inc(gn_dev_ready, 1)
                elif kind == "gn_var":
                    dve.wait_ge(ring_full, filled(dve, b, step))
                    dve.tensor_scalar(gve, ring_bank(b, step)[:, 0:1], GN_EPS, None, ALU.add)\
                        .then_inc(gn_var_ready, 1)
                elif kind == "gn_norm":
                    dve.wait_ge(gn_rstd_ready, at(dve, b, gn_rstd_ready, "gn_var"))
                    dve.tensor_tensor(se_in, gdev, grstd, ALU.mult).then_inc(se_in_ready, 1)
                elif kind == "se_in":
                    dve.wait_ge(ring_full, filled(dve, b, step))
                    dve.tensor_scalar(se_h[0:RED, :], ring_bank(b, step)[0:RED, 0:1], 0.0, None, ALU.max)\
                        .then_inc(se_hidden_ready, 1)
                elif kind == "se_out":
                    dve.wait_ge(se_exp_ready, at(dve, b, se_exp_ready, *step))
                    link(dve.tensor_scalar(se_tmp, se_e, 1.0, None, ALU.add))
                    dve.wait_ge(vector_chain, chained(b, step, links[0]))
                    link(dve.reciprocal(ysig, se_tmp))
                    dve.wait_ge(vector_chain, chained(b, step, links[0]))
                    link(dve.tensor_tensor(ysig, ysig, grstd, ALU.mult))
                    dve.wait_ge(vector_chain, chained(b, step, links[0]))
                    link(dve.tensor_scalar(yscale, ysig, 1.0, None, ALU.add))
                    link(dve.scalar_tensor_tensor(out=yshift, in0=gmean, scalar=-1.0, in1=ysig, op0=ALU.mult,
                                                  op1=ALU.mult))
                    dve.wait_ge(vector_chain, chained(b, step, links[0]))
                elif kind == "xgnorm":
                    u = step[1]
                    if u == 0 and b is not None:
                        dve.wait_ge(ring_full, filled(dve, b, ("pt", NB - 1, NT - 1)))
                    dve.tensor_scalar(xg_f[:, u, :], x_chan[:, u * LW:(u + 1) * LW], gmean, grstd,
                                      ALU.subtract, ALU.mult).then_inc(xg_norm_ready, 1)
                elif kind == "xg":
                    u = step[1]
                    dve.wait_ge(xg_norm_ready, at(dve, b, xg_norm_ready, "xgnorm", u))
                    dve.wait_ge(xg_hi_ready, at(dve, b, xg_hi_ready, *step))
                    if u == 0 and b is not None:
                        dve.wait_ge(s1_done, at(dve, b, s1_done, "s1", LB * NT - 1))
                    dve.tensor_tensor(xt_lo[:, u * LW:(u + 1) * LW], xg_f[:, u, :],
                                      xt_hi[:, u * LW:(u + 1) * LW], ALU.subtract).then_inc(xg_lo_ready, 1)
                elif kind == "kproj":
                    m = step[1]
                    dve.wait_ge(k_hi_ready, at(dve, b, k_hi_ready, *step))
                    dve.scalar_tensor_tensor(out=k_lo[:, m * BW:(m + 1) * BW], in0=key_bank(m),
                                             scalar=biases[:, 1:2], in1=k_hi[:, m * BW:(m + 1) * BW], op0=ALU.add,
                                             op1=ALU.subtract).then_inc(k_lo_ready, 1)
                elif kind == "qproj":
                    n = step[1]
                    dve.wait_ge(q_hi_ready, at(dve, b, q_hi_ready, *step))
                    dve.scalar_tensor_tensor(out=q_lo[:, n % 2, :], in0=ring_bank(b, step)[:, 0:BW],
                                             scalar=biases[:, 0:1], in1=q_hi[:, n % 2, :], op0=ALU.add,
                                             op1=ALU.subtract).then_inc(q_lo_ready, 1)
                elif kind == "vt":
                    m = step[1]
                    dve.wait_ge(v_hi_ready, at(dve, b, v_hi_ready, *step))
                    dve.tensor_tensor(v_lo[:, TPB * m:TPB * (m + 1), :], tiled(ring_bank(b, step)[:, 0:BW]),
                                      v_hi[:, TPB * m:TPB * (m + 1), :], ALU.subtract).then_inc(v_lo_ready, 1)
                elif kind == "scores":
                    n, r, c = step[1:]
                    dve.wait_ge(scores_done, at(dve, b, scores_done, *step))
                    link(dve.tensor_reduce(mx[:, c:c + 1], ps[:, c, 0:QC[c][1]], AX.X, ALU.max))
                elif kind == "row_max":
                    n, r = step[1:]
                    dve.wait_ge(vector_chain, chained(b, step, 0))
                    dve.tensor_reduce(negmax[:, r % 2:r % 2 + 1], mx[:, :], AX.X, ALU.max, negate=True)\
                        .then_inc(row_max_ready, 1)
                elif kind == "pt":
                    n, j = step[1:]
                    slot = (n * NT + j) % PTS
                    dve.wait_ge(pt_hi_ready, at(dve, b, pt_hi_ready, *step))
                    dve.tensor_tensor(pt_lo[:, slot, :], ring_bank(b, step)[:, 0:BW], pt_hi[:, slot, :],
                                      ALU.subtract).then_inc(pt_lo_ready, 1)
                elif kind == "rowsum":
                    m = step[1]
                    dve.wait_ge(p_rows_ready, at(dve, b, p_rows_ready, "exp", m, TPB - 1, len(QC) - 1))
                    link(dve.tensor_reduce(rg[:, 0, :], dparts[:, m, :, :], AX.X, ALU.add))
                    dve.wait_ge(vector_chain, chained(b, step, links[0]))
                    link(dve.reciprocal(rg[:, 1, :], rg[:, 0, :]))
                    dve.wait_ge(vector_chain, chained(b, step, links[0]))
                    link(dve.tensor_scalar(rg[:, 2, :], rg[:, 1, :], biases[:, 3:4], None, ALU.mult))
                    dve.wait_ge(vector_chain, chained(b, step, links[0]))
                elif kind == "ot":
                    m = step[1]
                    dve.wait_ge(ring_full, filled(dve, b, step))
                    dve.wait_ge(base_tok_ready, at(dve, b, base_tok_ready, "baset", m))
                    for k in range(TPB):
                        t = t_tok[:, TPB * m + k, :]
                        ins = dve.scalar_tensor_tensor(out=t, in0=ring_bank(b, step)[:, k * 128:(k + 1) * 128],
                                                       scalar=rg[:, 2, k:k + 1], in1=t, op0=ALU.mult, op1=ALU.add)
                        if k < TPB - 1:
                            link(ins)
                    ins.then_inc(o_added, 1)
                elif kind in ("ln", "uln"):
                    m = step[1]
                    raw, mv, ve = (ln_raw, ln_mv, ln_ve) if kind == "ln" else (u_raw, u_mv, u_ve)
                    src = t_tok
                    if kind == "ln":
                        dve.wait_ge(o_added, at(dve, b, o_added, "ot", m))
                    else:
                        dve.wait_ge(o1_added, at(dve, b, o1_added, "o1t", m))
                    for k in range(TPB):
                        link(dve.bn_stats(raw[:, k, :], src[:, TPB * m + k, :]))
                    dve.wait_ge(vector_chain, chained(b, step, links[0]))
                    dve.memset(wait_carrier[:, :], 0.0)
                    for k in range(TPB):
                        link(dve.bn_aggr(mv[:, k, :], raw[:, k, :]))
                    dve.wait_ge(vector_chain, chained(b, step, links[0]))
                    dve.tensor_scalar(ve[:, :], mv[:, :, 1], LN_EPS, None, ALU.add)\
                        .then_inc(ln_var_ready if kind == "ln" else u_var_ready, 1)
                elif kind in ("lnapply", "uapply"):
                    m = step[1]
                    mv, rs, dst = (ln_mv, ln_rs, tn_tok) if kind == "lnapply" else (u_mv, u_rs, u_tok)
                    if kind == "lnapply":
                        dve.wait_ge(ln_rstd_ready, at(dve, b, ln_rstd_ready, "ln", m))
                    else:
                        dve.wait_ge(u_rstd_ready, at(dve, b, u_rstd_ready, "uln", m))
                    if m >= 1:
                        dve.wait_ge(ring_full, filled(dve, b, ("tnt" if kind == "lnapply" else "ut", m - 1)))
                    for k in range(TPB):
                        ins = dve.tensor_scalar(dst[:, k, :], t_tok[:, TPB * m + k, :], mv[:, k, 0:1],
                                                rs[:, k:k + 1], ALU.subtract, ALU.mult)
                        if k < TPB - 1:
                            link(ins)
                    if kind == "uapply":
                        ins.then_inc(u_tok_ready, 1)
                    else:
                        ins.then_inc(tn_tok_ready, 1)
                elif kind == "lnlow":
                    m = step[1]
                    dve.wait_ge(tn_hi_ready, at(dve, b, tn_hi_ready, "lnhigh", m))
                    dve.scalar_tensor_tensor(out=tn_lo[:, TPB * m:TPB * (m + 1), :], in0=tn_tok[:, :, :], scalar=1.0,
                                             in1=tn_hi[:, TPB * m:TPB * (m + 1), :], op0=ALU.add,
                                             op1=ALU.subtract).then_inc(tn_lo_ready, 1)
                elif kind == "tnt":
                    m = step[1]
                    dve.wait_ge(tnt_hi_ready, at(dve, b, tnt_hi_ready, *step))
                    dve.tensor_tensor(xt_lo[:, m * BW:(m + 1) * BW], ring_bank(b, step)[:, 0:BW],
                                      xt_hi[:, m * BW:(m + 1) * BW], ALU.subtract).then_inc(tnt_lo_ready, 1)
                elif kind == "s1":
                    w = step[1]
                    dve.wait_ge(p1_hi_ready, at(dve, b, p1_hi_ready, *step))
                    dve.tensor_tensor(p1_lo[:, w % 3, :], p1_f[:, w % 2, :], p1_hi[:, w % 3, :],
                                      ALU.subtract).then_inc(p1_lo_ready, 1)
                elif kind == "o1t":
                    m = step[1]
                    dve.wait_ge(ring_full, filled(dve, b, step))
                    link(dve.tensor_reduce(r1[:, 0, :], tiled(ring_bank(b, step)[:, 0:BW]), AX.X, ALU.add))
                    dve.wait_ge(vector_chain, chained(b, step, links[0]))
                    link(dve.tensor_scalar(r1[:, 1, :], r1[:, 0, :], 1.0 / C, None, ALU.mult))
                    dve.wait_ge(vector_chain, chained(b, step, links[0]))
                    link(dve.reciprocal(r1[:, 2, :], r1[:, 1, :]))
                    dve.wait_ge(vector_chain, chained(b, step, links[0]))
                    for k in range(TPB):
                        t = t_tok[:, TPB * m + k, :]
                        ins = dve.scalar_tensor_tensor(out=t, in0=ring_bank(b, step)[:, k * 128:(k + 1) * 128],
                                                       scalar=r1[:, 2, k:k + 1], in1=t, op0=ALU.mult, op1=ALU.add)
                        if k < TPB - 1:
                            link(ins)
                    ins.then_inc(o1_added, 1)
                elif kind == "ut":
                    dve.wait_ge(u_hi_ready, at(dve, b, u_hi_ready, *step))
                    dve.tensor_tensor(u_lo[:, :], ring_bank(b, step)[:, 0:BW], u_hi[:, :],
                                      ALU.subtract).then_inc(u_lo_ready, 1)
                elif kind == "router":
                    m = step[1]
                    dve.wait_ge(ring_full, filled(dve, b, step))
                    shape = [128, TPB, E]
                    link(dve.tensor_tensor(logits[:, :, :],
                                           ring_bank(b, step)[:, 0:TPB * E].rearrange("p (t e) -> p t e", e=E),
                                           rb_sb[:, :].unsqueeze(1).broadcast_to(shape), ALU.add))
                    dve.wait_ge(vector_chain, chained(b, step, links[0]))
                    link(dve.tensor_reduce(lmax[:, :], logits[:, :, :], AX.X, ALU.max))
                    dve.wait_ge(vector_chain, chained(b, step, links[0]))
                    dve.tensor_tensor(centred[:, :, :], logits[:, :, :],
                                      lmax[:, :].unsqueeze(2).broadcast_to(shape),
                                      ALU.subtract).then_inc(logit_max_ready, 1)
                    own = logits[:, :, :].unsqueeze(3).broadcast_to([128, TPB, E, E])
                    other = logits[:, :, :].unsqueeze(2).broadcast_to([128, TPB, E, E])
                    low = lower[:, :, :].unsqueeze(1).broadcast_to([128, TPB, E, E])
                    link(dve.tensor_tensor(cmp_gt[:, :, :, :], other, own, ALU.is_gt))
                    link(dve.tensor_tensor(cmp_ge[:, :, :, :], other, own, ALU.is_ge))
                    dve.wait_ge(vector_chain, chained(b, step, links[0]))
                    link(dve.tensor_tensor(cmp_ge[:, :, :, :], cmp_ge[:, :, :, :], low, ALU.mult))
                    dve.wait_ge(vector_chain, chained(b, step, links[0]))
                    link(dve.tensor_tensor(cmp_gt[:, :, :, :], cmp_ge[:, :, :, :], cmp_gt[:, :, :, :], ALU.max))
                    dve.wait_ge(vector_chain, chained(b, step, links[0]))
                    link(dve.tensor_reduce(rank[:, :, :], cmp_gt[:, :, :, :], AX.X, ALU.add))
                    dve.wait_ge(vector_chain, chained(b, step, links[0]))
                    link(dve.tensor_scalar(rank[:, :, :], rank[:, :, :], 2.0, None, ALU.is_lt))
                    dve.wait_ge(vector_chain, chained(b, step, links[0]))
                    dve.wait_ge(gate_exp_ready, at(dve, b, gate_exp_ready, *step))
                    link(dve.tensor_tensor(gexp[:, :, :], gexp[:, :, :], rank[:, :, :], ALU.mult))
                    dve.wait_ge(vector_chain, chained(b, step, links[0]))
                    link(dve.tensor_reduce(gsum[:, 0, :], gexp[:, :, :], AX.X, ALU.add))
                    dve.wait_ge(vector_chain, chained(b, step, links[0]))
                    link(dve.reciprocal(gsum[:, 1, :], gsum[:, 0, :]))
                    dve.wait_ge(vector_chain, chained(b, step, links[0]))
                    dve.tensor_tensor(gates[:, m % 2, :, :], gexp[:, :, :],
                                      gsum[:, 1, :].unsqueeze(2).broadcast_to(shape),
                                      ALU.mult).then_inc(gates_ready, 1)
                elif kind == "expert":
                    m, k, half = step[1:]
                    dve.wait_ge(ring_full, filled(dve, b, step))
                    if k == 0 and half == 0:
                        dve.wait_ge(gates_ready, at(dve, b, gates_ready, "router", m))
                        if m >= 2:
                            dve.wait_ge(ring_full, filled(dve, b, ("yt", m - 2)))
                    if half == 1:
                        dve.wait_ge(expert_added, at(dve, b, expert_added, "expert", m, k, 0))
                    even, odd = acc[:, m % 2, k, :], acc_odd[:, :]
                    for e in range(E // 2):
                        i = half * (E // 2) + e
                        term = ring_bank(b, step)[:, e * 128:(e + 1) * 128]
                        gate = gates[:, m % 2, k, i:i + 1]
                        if e >= 2:
                            dve.wait_ge(vector_chain, chained(b, step, links[0] - 1))
                        if i == 1 and k:
                            dve.wait_ge(expert_added, at(dve, b, expert_added, "expert", m, k - 1, 1))
                        if i == 1:
                            ins = dve.tensor_scalar(odd, term, gate, None, ALU.mult)
                        else:
                            total = t_tok[:, TPB * m + k, :] if i == 0 else (even, odd)[i % 2]
                            ins = dve.scalar_tensor_tensor(out=(even, odd)[i % 2], in0=term, scalar=gate, in1=total,
                                                           op0=ALU.mult, op1=ALU.add)
                        if half == 0 and e == E // 2 - 1:
                            ins.then_inc(expert_added, 1)
                        else:
                            link(ins)
                    if half == 1:
                        dve.wait_ge(vector_chain, chained(b, step, links[0]))
                        dve.tensor_tensor(even, even, odd, ALU.add).then_inc(expert_added, 1)
                assert links[0] == linked(step), (kind, links[0])

            for step in HEAD:
                take(step, None)
            with dve.Fori(0, B) as b:
                for i, step in enumerate(PLAN):
                    here[dve.engine] = i
                    take(step, b)

        @block.tensor
        def _(pe):
            pe.sem_inc(pv1_done, 1)
            pe.wait_ge(w_split, W_SPLITS)
            pe.wait_ge(consts_made, 11)

            def three(out, lhs_hi, lhs_lo, rhs_hi, rhs_lo, start=True, stop=True):
                pe.matmul(out, lhs_hi, rhs_hi, start=start, stop=False)
                pe.matmul(out, lhs_hi, rhs_lo, start=False, stop=False)
                return pe.matmul(out, lhs_lo, rhs_hi, start=False, stop=stop)

            def transpose3(b, step, src):
                if b is not None or ring_index(b, step) >= 2:
                    pe.wait_ge(reader(b, step), freed(pe, b, step))
                for k in range(TPB):
                    ins = pe.transpose(ring_bank(b, step)[:, k * 128:(k + 1) * 128], src(k), ident[:, :])
                ins.then_inc(ring_full, 1)

            def project(out, m, w):
                cols = slice(m * BW, (m + 1) * BW)
                return three(out, w_hi[:, w, :], w_lo[:, w, :], xt_hi[:, cols], xt_lo[:, cols])

            def take(step, b):
                kind = step[0]
                if kind == "gn_dev":
                    if b is not None:
                        pe.wait_ge(reader(b, step), freed(pe, b, step))
                    pe.wait_ge(gn_stats_ready, at(pe, b, gn_stats_ready, "gn_mean"))
                    pe.matmul(ring_bank(b, step)[:, 0:1], group[:, :], gn_mv[:, 0:1], start=True, stop=True)\
                        .then_inc(ring_full, 1)
                elif kind == "gn_var":
                    if b is not None:
                        pe.wait_ge(reader(b, step), freed(pe, b, step))
                    pe.wait_ge(gn_dev_ready, at(pe, b, gn_dev_ready, "gn_dev"))
                    pe.matmul(ring_bank(b, step)[:, 0:1], group[:, :], gsq, start=True, stop=True)\
                        .then_inc(ring_full, 1)
                elif kind == "se_in":
                    pe.wait_ge(reader(b, step), freed(pe, b, step))
                    pe.wait_ge(se_in_ready, at(pe, b, se_in_ready, "gn_norm"))
                    pe.matmul(ring_bank(b, step)[0:RED, 0:1], w1_sb[:, :], se_in, start=True, stop=True)\
                        .then_inc(ring_full, 1)
                elif kind == "se_out":
                    pe.wait_ge(reader(b, step), freed(pe, b, step))
                    pe.wait_ge(se_hidden_ready, at(pe, b, se_hidden_ready, "se_in"))
                    pe.matmul(ring_bank(b, step)[:, 0:1], w2_sb[:, :], se_h[0:RED, :], start=True, stop=True)\
                        .then_inc(ring_full, 1)
                elif kind == "qproj":
                    m = step[1]
                    pe.wait_ge(xg_lo_ready, at(pe, b, xg_lo_ready, "xg", m // 2))
                    if b is not None or ring_index(b, step) >= 2:
                        pe.wait_ge(reader(b, step), freed(pe, b, step))
                    project(ring_bank(b, step)[:, 0:BW], m, 0).then_inc(ring_full, 1)
                elif kind == "kproj":
                    m = step[1]
                    pe.wait_ge(xg_lo_ready, at(pe, b, xg_lo_ready, "xg", m // 2))
                    if m == 0 and b is not None:
                        pe.wait_ge(p1_exp_ready, at(pe, b, p1_exp_ready, "s1", LB * NT - 1))
                    if m == 4 and b is not None:
                        pe.wait_ge(o1_chan_ready, at(pe, b, o1_chan_ready, "o1evac", LB - 1))
                    if m == 5:
                        pe.wait_ge(k_lo_ready, at(pe, b, k_lo_ready, "kproj", 0))
                    project(key_bank(m), m, 1).then_inc(kproj_done, 1)
                elif kind == "vproj":
                    m = step[1]
                    pe.wait_ge(xg_lo_ready, at(pe, b, xg_lo_ready, "xg", m // 2))
                    if m:
                        pe.wait_ge(v_chan_ready, at(pe, b, v_chan_ready, "vproj", m - 1))
                    elif b is not None:
                        pe.wait_ge(o1_chan_ready, at(pe, b, o1_chan_ready, "o1evac", LB - 1))
                    project(ps[:, 5, 0:BW], m, 2).then_inc(vproj_done, 1)
                elif kind == "vt":
                    m = step[1]
                    pe.wait_ge(v_chan_ready, at(pe, b, v_chan_ready, "vproj", m))
                    transpose3(b, step, lambda k: v_chan[:, m % 2, k * 128:(k + 1) * 128])
                elif kind == "baset":
                    m = step[1]
                    pe.wait_ge(base_done, at(pe, b, base_done, "base", m // 2))
                    transpose3(b, step, lambda k: x_chan[:, m * BW + k * 128:m * BW + (k + 1) * 128])
                elif kind == "scores":
                    n, r, c = step[1:]
                    if c == 0 and r == 0:
                        pe.wait_ge(q_lo_ready, at(pe, b, q_lo_ready, "qproj", n))
                        if n == 0:
                            pe.wait_ge(k_lo_ready, at(pe, b, k_lo_ready, "kproj", NB - 1))
                    row = n * TPB + r
                    if row:
                        pe.wait_ge(p_rows_ready, at(pe, b, p_rows_ready, "exp", (row - 1) // TPB, (row - 1) % TPB, c))
                    a, w = QC[c]
                    tile = slice(r * 128, (r + 1) * 128)
                    three(ps[:, c, 0:w], q_hi[:, n % 2, tile], q_lo[:, n % 2, tile], k_hi[:, a:a + w],
                          k_lo[:, a:a + w]).then_inc(scores_done, 1)
                elif kind == "pt":
                    n, j = step[1:]
                    pe.wait_ge(p_rows_ready, at(pe, b, p_rows_ready, "exp", n, TPB - 1, chunk_of(j)))
                    transpose3(b, step, lambda k: p_rows[:, ROW_BUFFER[k, n % 2], j * 128:(j + 1) * 128])
                elif kind == "pv":
                    n, j = step[1:]
                    slot = (n * NT + j) % PTS
                    pe.wait_ge(pt_lo_ready, at(pe, b, pt_lo_ready, "pt", n, j))
                    if j == 0:
                        if n:
                            pe.wait_ge(o_chan_ready, at(pe, b, o_chan_ready, "oevac", n - 1))
                        else:
                            pe.wait_ge(v_lo_ready, at(pe, b, v_lo_ready, "vt", NB - 1))
                            pe.wait_ge(o1_chan_ready, before(pe, b, o1_chan_ready))
                    three(ps[:, 5, 0:BW], v_hi[:, j, :], v_lo[:, j, :], pt_hi[:, slot, :], pt_lo[:, slot, :],
                          start=j == 0, stop=j == NT - 1).then_inc(pv_done, 1)
                elif kind == "ot":
                    pe.wait_ge(o_chan_ready, at(pe, b, o_chan_ready, "oevac", step[1]))
                    transpose3(b, step, lambda k: o_chan[:, k * 128:(k + 1) * 128])
                elif kind == "tnt":
                    pe.wait_ge(tn_tok_ready, at(pe, b, tn_tok_ready, "lnapply", step[1]))
                    transpose3(b, step, lambda k: tn_tok[:, k, :])
                elif kind == "s1":
                    w = step[1]
                    ib, j = divmod(w, NT)
                    if ib == 0:
                        pe.wait_ge(tnt_lo_ready, at(pe, b, tnt_lo_ready, "tnt", max(j // TPB, 1)))
                    if w >= 2:
                        pe.wait_ge(p1_exp_ready, at(pe, b, p1_exp_ready, "s1", w - 2))
                    else:
                        pe.wait_ge(p_rows_ready, at(pe, b, p_rows_ready, "exp", NB - 1, TPB - 1, 3))
                    tile = slice(j * 128, (j + 1) * 128)
                    for i in range(2):
                        cols = slice(ib * LW + i * BW, ib * LW + (i + 1) * BW)
                        ins = three(ps[:, 2 * (w % 2) + i, 0:BW], xt_hi[:, tile], xt_lo[:, tile], xt_hi[:, cols],
                                    xt_lo[:, cols])
                    ins.then_inc(s1_done, 1)
                elif kind == "pv1":
                    w = step[1]
                    ib, j = divmod(w, NT)
                    pe.wait_ge(p1_lo_ready, at(pe, b, p1_lo_ready, "s1", w))
                    if ib == 0:
                        pe.wait_ge(tn_lo_ready, at(pe, b, tn_lo_ready, "lnlow", j // TPB))
                    if j == 0:
                        if ib:
                            pe.wait_ge(o1_chan_ready, at(pe, b, o1_chan_ready, "o1evac", ib - 1))
                        else:
                            pe.wait_ge(o_chan_ready, at(pe, b, o_chan_ready, "oevac", NB - 1))
                            pe.wait_ge(p_rows_ready, at(pe, b, p_rows_ready, "exp", NB - 1, TPB - 1, 4))
                    for i in range(2):
                        cols = slice(i * BW, (i + 1) * BW)
                        ins = three(ps[:, 4 + i, 0:BW], tn_hi[:, j, :], tn_lo[:, j, :],
                                    p1_hi[:, w % 3, cols], p1_lo[:, w % 3, cols], start=j == 0, stop=j == NT - 1)
                    ins.then_inc(pv1_done, 1)
                elif kind == "o1t":
                    m = step[1]
                    pe.wait_ge(o1_chan_ready, at(pe, b, o1_chan_ready, "o1evac", m // 2))
                    transpose3(b, step, lambda k: o1_chan[:, (m // 2) % 2, (m % 2 * TPB + k) * 128:
                                                        (m % 2 * TPB + k + 1) * 128])
                elif kind == "ut":
                    pe.wait_ge(u_tok_ready, at(pe, b, u_tok_ready, "uapply", step[1]))
                    transpose3(b, step, lambda k: u_tok[:, k, :])
                elif kind == "router":
                    m = step[1]
                    pe.wait_ge(u_lo_ready, at(pe, b, u_lo_ready, "ut", m))
                    pe.wait_ge(reader(b, step), freed(pe, b, step))
                    for k in range(TPB):
                        tile = slice(k * 128, (k + 1) * 128)
                        out = ring_bank(b, step)[:, k * E:(k + 1) * E]
                        pe.matmul(out, u_lo[:, tile], rw_lo[:, :], start=True, stop=False)
                        pe.matmul(out, u_hi[:, tile], rw_lo[:, :], start=False, stop=False)
                        pe.matmul(out, u_lo[:, tile], rw_hi[:, :], start=False, stop=False)
                        ins = pe.matmul(out, u_hi[:, tile], rw_hi[:, :], start=False, stop=True)
                    ins.then_inc(ring_full, 1)
                elif kind == "expert":
                    m, k, half = step[1:]
                    pe.wait_ge(reader(b, step), freed(pe, b, step))
                    tile = slice(k * 128, (k + 1) * 128)
                    cols = slice(half * 512, (half + 1) * 512)
                    out = ring_bank(b, step)
                    pe.matmul(out, ones[0:64, :], eb_rows[0:64, cols], start=True, stop=False)
                    three(out, u_hi[:, tile], u_lo[:, tile], ew_hi[:, cols], ew_lo[:, cols], start=False)\
                        .then_inc(ring_full, 1)
                elif kind == "yt":
                    m = step[1]
                    pe.wait_ge(expert_added, at(pe, b, expert_added, "expert", m, TPB - 1, 1))
                    transpose3(b, step, lambda k: acc[:, m % 2, k, :])

            for step in HEAD:
                take(step, None)
            with pe.Fori(0, B) as b:
                for i, step in enumerate(PLAN):
                    here[pe.engine] = i
                    take(step, b)



_INS = ["x", "wq", "wk", "wv", "bq", "bk", "bv", "w1", "w2", "gamma", "rw", "rb", "ew", "eb"]


def kernel(x, L0_conv_Wq, L0_conv_bq, L0_conv_Wk, L0_conv_bk, L0_conv_Wv, L0_conv_bv, L0_conv_se_w1, L0_conv_se_w2,
           L0_conv_gamma, L1_ffn_router_w, L1_ffn_router_b, L1_ffn_expert_w, L1_ffn_expert_b):
    import numpy as np
    import concourse.bacc as bacc
    from concourse.bass_utils import run_bass_kernel_spmd

    laid = {
        "x": np.asarray(x).reshape(B, C, NTOK),
        "wq": np.asarray(L0_conv_Wq).T, "wk": np.asarray(L0_conv_Wk).T, "wv": np.asarray(L0_conv_Wv).T,
        "bq": np.asarray(L0_conv_bq).reshape(C, 1), "bk": np.asarray(L0_conv_bk).reshape(C, 1),
        "bv": np.asarray(L0_conv_bv).reshape(C, 1),
        "w1": np.asarray(L0_conv_se_w1).T, "w2": np.asarray(L0_conv_se_w2).T,
        "gamma": np.broadcast_to(np.asarray(L0_conv_gamma).reshape(1, 1), (C, 1)),
        "rw": np.asarray(L1_ffn_router_w),
        "rb": np.broadcast_to(np.asarray(L1_ffn_router_b).reshape(1, E), (C, E)),
        "ew": np.asarray(L1_ffn_expert_w).transpose(1, 0, 2).reshape(C, E * C),
        "eb": np.asarray(L1_ffn_expert_b).reshape(1, E * C),
    }
    nc = bacc.Bacc("TRN2", target_bir_lowering=False, num_devices=1)
    arrays, args = {}, []
    for name in _INS:
        arrays[name] = np.ascontiguousarray(laid[name])
        args.append(nc.dram_tensor(name, arrays[name].shape, F32, kind="ExternalInput").ap())
    out = nc.dram_tensor("y", (B, C, NTOK), F32, kind="ExternalOutput").ap()
    build(nc, *args, out)
    r = run_bass_kernel_spmd(nc, [arrays], core_ids=[0])
    return r.results[0]["y"].reshape(B, C, 48, 48)
```
